# Optimizing a Trainium2 kernel written in Bass

```python
import numpy as np
import jax
import jax.numpy as jnp

def _softmax(x, axis=-1):
    return jax.nn.softmax(x, axis=axis)

def _gelu(x):
    return jax.nn.gelu(x, approximate=True)

def _silu(x):
    return jax.nn.silu(x)

def _sigmoid(x):
    return jax.nn.sigmoid(x)

def _layernorm(x, axis=-1, eps=1e-05):
    m = jnp.mean(x, axis=axis, keepdims=True)
    v = jnp.var(x, axis=axis, keepdims=True)
    return (x - m) / jnp.sqrt(v + eps)

def _scatter_add(tgt, idx, src, axis=0):
    return tgt.at[idx].add(src)

def _segment_sum(src, seg, n):
    return jax.ops.segment_sum(src, seg, n)
kernel_name = 'mk_xattn_ffn_d1_seqx_r4_9fed02'

def setup_inputs(seed: int=0):
    np.random.seed(seed)
    _w = jnp.asarray

    def _rec_inputs():
        import jax
        import jax.numpy as jnp
        _rk = jax.random.key(seed)
        x = -0.0002928 + 1 * jax.random.normal(jax.random.fold_in(_rk, 1), (2, 1024, 256), jnp.float32)
        _lenS = 1024 - jax.random.randint(jax.random.fold_in(_rk, 7), (2,), 0, max(1, 1024 // 4) + 1, jnp.int32)
        _lenS2 = 77 - jax.random.randint(jax.random.fold_in(_rk, 8), (2,), 0, max(1, 77 // 4) + 1, jnp.int32)
        _ctx_1024P = jax.random.normal(jax.random.fold_in(_rk, 11), (2, 16, 256), jnp.float32)
        _ctx_1024c = jax.random.dirichlet(jax.random.fold_in(_rk, 511), 0.3 * jnp.ones((16,), jnp.float32), (2, 77))
        _ctx_1024t = jnp.einsum('bsk,bkd->bsd', _ctx_1024c, _ctx_1024P)
        _ctx_1024t = _ctx_1024t * jax.lax.rsqrt(jnp.mean(jnp.square(_ctx_1024t)) + 1e-12) * 0.953939
        ctx_1024 = -1.39393e-06 + 0.999914 * (_ctx_1024t + 0.3 * jax.random.normal(jax.random.fold_in(_rk, 611), (2, 77, 256), jnp.float32))
        return (x, ctx_1024)
    x, ctx_1024 = _rec_inputs()

    def _L0_xattn_setup():
        import jax, jax.numpy as jnp
        import numpy as np
        B, N, M = (2, 512, 512)
        Q_DIM = 256
        HEADS = 8
        DIM_HEAD = 64
        INNER = HEADS * DIM_HEAD
        key = jax.random.key(seed)
        ks = jax.random.split(key, 7)
        s_in = 1.0 / np.sqrt(Q_DIM)
        s_out = 1.0 / np.sqrt(INNER)
        return {'x': jax.random.normal(ks[0], (B, N, Q_DIM), dtype=jnp.float32), 'context': jax.random.normal(ks[1], (B, M, Q_DIM), dtype=jnp.float32), 'Wq': jax.random.normal(ks[2], (Q_DIM, INNER), dtype=jnp.float32) * s_in, 'Wk': jax.random.normal(ks[3], (Q_DIM, INNER), dtype=jnp.float32) * s_in, 'Wv': jax.random.normal(ks[4], (Q_DIM, INNER), dtype=jnp.float32) * s_in, 'Wo': jax.random.normal(ks[5], (INNER, Q_DIM), dtype=jnp.float32) * s_out, 'bo': jax.random.normal(ks[6], (Q_DIM,), dtype=jnp.float32) * 0.01}
    _L0_xattn_all = _L0_xattn_setup()
    _L0_xattn_in = {k: v for k, v in _L0_xattn_all.items() if k in ('Wq', 'Wk', 'Wv', 'Wo', 'bo')}
    del _L0_xattn_all

    def _L0_ffn_setup():
        import jax, jax.numpy as jnp
        import numpy as np
        DIM = 256
        MOE_HID = 128
        SHARED_HID = 512
        N_EXPERTS = 16
        TOP_K = 2
        NORM_TOPK_PROB = True
        key = jax.random.key(seed)
        ks = jax.random.split(key, 9)
        s = 0.02
        x = jax.random.normal(ks[0], (2, 256, DIM), dtype=jnp.float32)
        Wg = jax.random.normal(ks[1], (N_EXPERTS, DIM), dtype=jnp.float32) * s
        We_gate = jax.random.normal(ks[2], (N_EXPERTS, MOE_HID, DIM), dtype=jnp.float32) * s
        We_up = jax.random.normal(ks[3], (N_EXPERTS, MOE_HID, DIM), dtype=jnp.float32) * s
        We_down = jax.random.normal(ks[4], (N_EXPERTS, DIM, MOE_HID), dtype=jnp.float32) * s
        Ws_gate = jax.random.normal(ks[5], (SHARED_HID, DIM), dtype=jnp.float32) * s
        Ws_up = jax.random.normal(ks[6], (SHARED_HID, DIM), dtype=jnp.float32) * s
        Ws_down = jax.random.normal(ks[7], (DIM, SHARED_HID), dtype=jnp.float32) * s
        Wsg = jax.random.normal(ks[8], (1, DIM), dtype=jnp.float32) * s
        return {'x': x, 'Wg': Wg, 'We_gate': We_gate, 'We_up': We_up, 'We_down': We_down, 'Ws_gate': Ws_gate, 'Ws_up': Ws_up, 'Ws_down': Ws_down, 'Wsg': Wsg}
    _L0_ffn_all = _L0_ffn_setup()
    _L0_ffn_in = {k: v for k, v in _L0_ffn_all.items() if k in ('Wg', 'We_gate', 'We_up', 'We_down', 'Ws_gate', 'Ws_up', 'Ws_down', 'Wsg')}
    del _L0_ffn_all
    return {'x': x, 'ctx_1024': ctx_1024, 'L0_xattn_Wq': _L0_xattn_in['Wq'], 'L0_xattn_Wk': _L0_xattn_in['Wk'], 'L0_xattn_Wv': _L0_xattn_in['Wv'], 'L0_xattn_Wo': _L0_xattn_in['Wo'], 'L0_xattn_bo': _L0_xattn_in['bo'], 'L0_ffn_Wg': _L0_ffn_in['Wg'], 'L0_ffn_We_gate': _L0_ffn_in['We_gate'], 'L0_ffn_We_up': _L0_ffn_in['We_up'], 'L0_ffn_We_down': _L0_ffn_in['We_down'], 'L0_ffn_Ws_gate': _L0_ffn_in['Ws_gate'], 'L0_ffn_Ws_up': _L0_ffn_in['Ws_up'], 'L0_ffn_Ws_down': _L0_ffn_in['Ws_down'], 'L0_ffn_Wsg': _L0_ffn_in['Wsg']}

def reference(x, ctx_1024, L0_xattn_Wq, L0_xattn_Wk, L0_xattn_Wv, L0_xattn_Wo, L0_xattn_bo, L0_ffn_Wg, L0_ffn_We_gate, L0_ffn_We_up, L0_ffn_We_down, L0_ffn_Ws_gate, L0_ffn_Ws_up, L0_ffn_Ws_down, L0_ffn_Wsg):
    import jax
    import jax.numpy as jnp

    def _L0_xattn_ref(x, context, Wq, Wk, Wv, Wo, bo):
        import jax, jax.numpy as jnp
        import numpy as np
        B, N, M = (2, 512, 512)
        Q_DIM = 256
        HEADS = 8
        DIM_HEAD = 64
        INNER = HEADS * DIM_HEAD
        scale = DIM_HEAD ** (-0.5)

        def split_heads(t):
            b, n, _ = t.shape
            return t.reshape(b, n, HEADS, DIM_HEAD).transpose(0, 2, 1, 3)
        q = split_heads(x @ Wq)
        k = split_heads(context @ Wk)
        v = split_heads(context @ Wv)
        sim = jnp.einsum('bhid,bhjd->bhij', q, k) * scale
        attn = jax.nn.softmax(sim, axis=-1)
        out = jnp.einsum('bhij,bhjd->bhid', attn, v)
        out = out.transpose(0, 2, 1, 3).reshape(x.shape[0], x.shape[1], INNER)
        return out @ Wo + bo

    def _L0_ffn_ref(x, Wg, We_gate, We_up, We_down, Ws_gate, Ws_up, Ws_down, Wsg):
        import jax, jax.numpy as jnp
        import numpy as np
        DIM = 256
        MOE_HID = 128
        SHARED_HID = 512
        N_EXPERTS = 16
        TOP_K = 2
        NORM_TOPK_PROB = True
        B, S, D = x.shape
        xt = x.reshape(-1, D)
        gates = jax.nn.softmax(xt @ Wg.T, axis=-1)
        scores, inds = jax.lax.top_k(gates, TOP_K)
        if NORM_TOPK_PROB:
            scores = scores / jnp.sum(scores, axis=-1, keepdims=True)
        g = jnp.einsum('td,ehd->teh', xt, We_gate)
        u = jnp.einsum('td,ehd->teh', xt, We_up)
        h = jax.nn.silu(g) * u
        y_all = jnp.einsum('teh,edh->ted', h, We_down)
        y_sel = jnp.take_along_axis(y_all, inds[:, :, None], axis=1)
        y = jnp.sum(y_sel * scores[:, :, None], axis=1)
        shared = jax.nn.silu(xt @ Ws_gate.T) * (xt @ Ws_up.T) @ Ws_down.T
        y = y + jax.nn.sigmoid(xt @ Wsg.T) * shared
        return y.reshape(B, S, D)
    x = x + _L0_xattn_ref(_layernorm(x, axis=-1), ctx_1024, L0_xattn_Wq, L0_xattn_Wk, L0_xattn_Wv, L0_xattn_Wo, L0_xattn_bo)
    x = x + _L0_ffn_ref(_layernorm(x, axis=-1), L0_ffn_Wg, L0_ffn_We_gate, L0_ffn_We_up, L0_ffn_We_down, L0_ffn_Ws_gate, L0_ffn_Ws_up, L0_ffn_Ws_down, L0_ffn_Wsg)
    return x

_drawn_inputs = setup_inputs


def setup_inputs(seed=0):
    import zlib

    import numpy as np

    out = dict(_drawn_inputs(seed))
    spreads = {}
    factors = {'L0_xattn_bo': 6.219,
     'L0_ffn_Wg': 8.0,
     'L0_ffn_We_gate': 7.671,
     'L0_ffn_We_up': 7.594,
     'L0_ffn_We_down': 7.592,
     'L0_ffn_Ws_gate': 5.737,
     'L0_ffn_Ws_up': 5.562,
     'L0_ffn_Ws_down': 5.573,
     'L0_ffn_Wsg': 8.0}
    for name, (base, spread) in spreads.items():
        noise = np.random.default_rng([zlib.crc32(name.encode()), seed]).standard_normal(out[name].shape)
        drawn = base * np.exp(spread * noise) if base else spread * noise
        out[name] = jnp.asarray(drawn.astype(out[name].dtype))
    for name, factor in factors.items():
        out[name] = (out[name] * factor).astype(out[name].dtype)
    return out
```

```python
from contextlib import ExitStack

import concourse.bass as bass
from concourse import mybir

ALU = mybir.AluOpType
ACT = mybir.ActivationFunctionType
AX = mybir.AxisListType.X
F32 = mybir.dt.float32
BF16 = mybir.dt.bfloat16
I32 = mybir.dt.int32
U32 = mybir.dt.uint32

P = 128
BANK = 512
RING = 4
LN_EPS = 1e-5
RSQRT_MAGIC = 0x5F3759DF
NEWTON = 3
MASKED = -3.0e38


def build(nc, x, ctx_t, wk, wv, wq_t, wo, bo, w_router, w_expert, w_shared_in, w_shared_out, out):
    B, N, D = x.shape
    KD = D // P
    INNER = wk.shape[1]
    PAIRS = INNER // P
    M = ctx_t.shape[1] // B
    H = 2 * PAIRS
    HM = H * M
    HALF = HM // 2
    HH = H // 2
    KEYS = [min(P, HM - c) for c in range(0, HM, P)]
    KC = len(KEYS)
    SCALE = float(INNER // H) ** -0.5
    TB = N // P
    T = B * TB
    E = w_expert.shape[0]
    EW = w_expert.shape[2]
    NR = w_router.shape[1]
    SJ = w_shared_out.shape[0] // P
    SHID = SJ * P
    G4 = 4
    GT = G4 * P
    ET = 2 * T + E - 1
    SCORE_W = NR + 1

    xs_dram = nc.dram_tensor("tokens_by_expert", (ET * P, D), F32, kind="Internal").ap()
    ys_dram = nc.dram_tensor("results_by_expert", (ET * P, D), F32, kind="Internal").ap()

    with ExitStack() as ctx:
        def sb(name, shape, dt=F32):
            return ctx.enter_context(nc.sbuf_tensor(name, shape, dt))

        def psum(name, shape):
            return ctx.enter_context(nc.psum_tensor(name, shape, F32))

        def sem(name):
            return ctx.enter_context(nc.semaphore(name))

        x_all = sb("x_all", [P, T, D])
        xn2_all = sb("xn2_all", [P, T, D])
        x2t_all = sb("x2t_all", [P, KD, T * P])
        scratch = sb("scratch", [P, PAIRS * B * KC * P])
        ctx_sb = sb("ctx_sb", [P, KD, B * M])
        attn_w = sb("attn_w", [P, 4, KD * INNER])
        bo_sb = sb("bo_sb", [P, D])
        kt_sb = sb("kt_sb", [P, PAIRS, B, 2, M])
        folded = sb("folded", [P, B * KD * HM + B * KC * D])
        wr_sb = sb("wr_sb", [P, KD, NR])
        we_sb = sb("we_sb", [P, E, EW])
        wsi_sb = sb("wsi_sb", [P, KD, 2 * SHID])
        wso_sb = sb("wso_sb", [P, SJ, D])
        ident = sb("ident", [P, P])
        zeros = sb("zeros", [P, D])
        stats = sb("stats", [P, T, 6])
        moments1 = sb("moments1", [P, T, 2])
        var1 = sb("var1", [P, T])
        rstd1 = sb("rstd1", [P, T])
        newton1 = sb("newton1", [P, T])
        stats2 = sb("stats2", [P, 6])
        moments2 = sb("moments2", [P, 2, 2])
        var2 = sb("var2", [P, 2])
        half2 = sb("half2", [P, 2])
        rstd2 = sb("rstd2", [P, 2])
        newton2 = sb("newton2", [P, 2])
        xn1 = sb("xn1", [P, 2, D])
        xt = sb("xt", [P, 2, KD, P])
        xn2 = sb("xn2", [P, 2, D])
        smax = sb("smax", [P, 2, H])
        ssum = sb("ssum", [P, 2, H])
        srec = sb("srec", [P, 2, H])
        probs = sb("probs", [P, 2, HM])
        pt_sb = sb("pt_sb", [P, KC, P])
        th = sb("th", [P, 2, GT])
        ga = sb("ga", [P, 2, GT])
        lg = sb("lg", [P, T, NR])
        lg2 = sb("lg2", [P, T, E])
        eq = sb("eq", [P, T, E])
        oh1 = sb("oh1", [P, T, E])
        oh2 = sb("oh2", [P, T, E])
        top1 = sb("top1", [P, T])
        top2 = sb("top2", [P, T])
        pick = sb("pick", [P, T])
        picked = sb("picked", [P, T, E], BF16)
        picked_t = sb("picked_t", [P, E], BF16)
        earlier = sb("earlier", [P, P], BF16)
        ones = sb("ones", [P, P], BF16)
        rank_first = sb("rank_first", [P, E])
        step_rows = sb("step_rows", [P, T])
        before = sb("before", [P, E, E])
        tile_no = sb("tile_no", [1, ET])
        counts = sb("counts", [P, E])
        ntiles = sb("ntiles", [P, E])
        base = sb("base", [P, E])
        base_end = sb("base_end", [P, E])
        base_row = sb("base_row", [P, E])
        past = sb("past", [1, ET, E])
        ewf = sb("ewf", [1, ET])
        expert_off = sb("expert_off", [1, ET], I32)
        posf = sb("posf", [P, 2, T])
        pos = sb("pos", [P, 2, T], U32)
        w12 = sb("w12", [P, 2, T])
        gap = sb("gap", [P, T])
        egap = sb("egap", [P, T])
        tgate = sb("tgate", [P, T])
        sgate = sb("sgate", [P, T])

        quad = psum("quad", [P, 2, 2, BANK])
        turned = psum("turned", [P, 2, BANK])
        result = psum("result", [P, 2, BANK])
        turned_flat = turned[:, :, :].rearrange("p a n -> p (a n)")
        result_x = result[:, 0, 0:D]

        vt_sb = scratch[:, :].rearrange("p (j b c) -> p j b c", j=PAIRS, b=B)
        second = scratch[:, 0:T * D].rearrange("p (t d) -> p t d", t=T)
        g_sb = folded[:, 0:B * KD * HM].rearrange("p (b k n) -> p b k n", b=B, k=KD)
        vo_sb = folded[:, B * KD * HM:].rearrange("p (b c n) -> p b c n", b=B, c=KC)
        at = [0]

        def part(n, size):
            view = folded[:, at[0]:at[0] + n * size].rearrange("p (n c) -> p n c", n=n)
            at[0] += n * size
            return view

        xs, ys = part(RING, D), part(RING, D)
        xst = part(2, KD * P).rearrange("p n (k c) -> p n k c", k=KD)
        eth, ega, eh, eht = part(2, P), part(2, P), part(2, P), part(2, P)
        first = xn2_all
        lt_sb = scratch[0:NR, 0:T * P]
        wk_sb = attn_w[:, 0, :].rearrange("p (k n) -> p k n", k=KD)
        wv_sb = attn_w[:, 1, :].rearrange("p (k n) -> p k n", k=KD)
        wqt_sb = attn_w[:, 2, :].rearrange("p (j n) -> p j n", j=PAIRS)
        wo_sb = attn_w[:, 3, :].rearrange("p (j n) -> p j n", j=PAIRS)
        hs = attn_w[:, :, :].rearrange("p a (b n) -> p (a b) n", n=GT).rearrange("p (g j) n -> p g j n", g=2)

        names = """kv_w_in wv_in wq_in wo_in bo_in wr_in ws_in we_in zero_filled zeros_set blocks_cleared
            ident_cleared ident_set kt_in_ps kt_set vt_in_ps vt_set g_in_ps g_set_dve g_set_act vo_in_ps vo_set
            dve_link pool_link consts_set
            xn1_set x_biased xt_in_ps xt_set scores_in_ps max_found shifted exps_set summed recip_set probs_set
            pt_in_ps pt_set_act pt_set_dve attn_in_ps x2_set stats2_set moments2_set var2_set guess2_set
            rstd2_set xn2_set xn2t_in_ps xn2t_set
            lt_in_ps lt_set logits_in_ps picked_set picked_t_set ranks_in_ps counts_in_ps gaps_set egap_set tgate_set
            pos_set experts_set weights_set scattered
            gate_in_ps up_in_ps tanh_set ga_set hs_set down_in_ps shared_added
            xst_in_ps xst_set gu_in_ps eth_set ega_set eh_set eht_in_ps eht_set y_in_ps ys_set
            first_added combined out_stored""".split()
        S = {n: sem(n) for n in names}
        x_in = [sem(f"x_in{c}") for c in range(T // G4)]
        xn2_saved = [sem(f"xn2_saved{c}") for c in range(2)]
        xs_in = [sem(f"xs_in{c}") for c in range(RING)]
        ys_stored = [sem(f"ys_stored{c}") for c in range(RING)]
        gathered = [sem(f"gathered{t}") for t in range(T)]

        def g_ps(n):
            return quad[:, n, :, :] if n < KD else result[:, :, :]

        def vt_ps(j):
            return (turned if j < 2 else result)[:, j % 2, 0:B * M]

        def vo_ps(n):
            return (turned if n % 2 else result)[:, 0, 0:D]

        def rows(ap):
            return ap.rearrange("b (p t) d -> p b t d", p=P)

        LOOP0, LOOP1 = 2, T - 4

        def tile_loop(eng, body):
            with eng.Fori(0, (LOOP1 - LOOP0) // 2) as i:
                for c in range(2):
                    body(i * 2 + (LOOP0 + c), c)

        ELOOP = (ET - 3) // RING * RING

        def expert_loop(eng, body):
            with eng.Fori(0, ELOOP // RING) as i:
                for c in range(RING):
                    body(i * RING + c, c, i)

        def apart(eng):
            eng.wait_ge(S["zeros_set"], 1)

        block = ctx.enter_context(nc.Block())

        @block.sync
        def _(sp):
            sp.dma_start(ctx_sb[:, :, :], ctx_t.rearrange("(k p) m -> p k m", p=P)).then_inc(S["kv_w_in"], 16)
            sp.dma_start(wk_sb[:, :, :], wk.rearrange("(k p) n -> p k n", p=P)).then_inc(S["kv_w_in"], 16)
            sp.dma_start(wqt_sb[:, :, :], wq_t.rearrange("(j p) n -> p j n", p=P)).then_inc(S["wq_in"], 16)
            sp.dma_start(wv_sb[:, :, :], wv.rearrange("(k p) n -> p k n", p=P)).then_inc(S["wv_in"], 16)
            sp.dma_start(wo_sb[:, :, :], wo.rearrange("(j p) n -> p j n", p=P)).then_inc(S["wo_in"], 16)
            sp.dma_start(wr_sb[:, :, :], w_router.rearrange("(k p) n -> p k n", p=P)).then_inc(S["wr_in"], 16)
            sp.dma_start(wsi_sb[:, :, :], w_shared_in.rearrange("(k p) n -> p k n", p=P)).then_inc(S["ws_in"], 16)
            sp.dma_start(wso_sb[:, :, :], w_shared_out.rearrange("(j p) n -> p j n", p=P)).then_inc(S["ws_in"], 16)
            sp.wait_ge(S["zeros_set"], 1)
            sp.dma_start(xs_dram.rearrange("(r p) d -> p r d", p=P),
                         zeros[:, :].unsqueeze(1).to_broadcast([P, ET, D])).then_inc(S["zero_filled"], 16)
            sp.dma_start(we_sb[:, :, :], w_expert.rearrange("e p n -> p e n")).then_inc(S["we_in"], 16)

            def save(t, par):
                sp.wait_ge(S["xn2_set"], t + 1)
                sp.dma_start(xn2_all[:, t, :], xn2[:, par, :]).then_inc(xn2_saved[par], 16)

            for t in range(LOOP0):
                save(t, t % 2)
            tile_loop(sp, save)
            for t in range(LOOP1, T):
                save(t, t % 2)

            sp.wait_ge(S["scattered"], 16 * 2 * T)
            for t in range(RING):
                sp.dma_start(xs[:, t, :], xs_dram[t * P:(t + 1) * P, :]).then_inc(xs_in[t], 16)

            def load(t, slot):
                sp.wait_ge(S["xst_in_ps"], t + 1)
                sp.dma_start(xs[:, slot, :], xs_dram[bass.ds((t + RING) * P, P), :]).then_inc(xs_in[slot], 16)

            def store(t, slot):
                sp.wait_ge(S["ys_set"], t + 1)
                sp.dma_start(ys_dram[bass.ds(t * P, P), :], ys[:, slot, :]).then_inc(ys_stored[slot], 16)

            with sp.Fori(0, ELOOP // RING - 1) as i:
                for c in range(RING):
                    load(i * RING + c, c)
                    store(i * RING + c, c)
            for t in range(ELOOP - RING, ET):
                if t + RING < ET:
                    load(t, t % RING)
                store(t, t % RING)

            out_rows = rows(out)
            for t in range(1, T, 2):
                sp.wait_ge(S["combined"], t + 1)
                b, tb = t // TB, t % TB
                sp.dma_start(out_rows[:, b, tb - 1:tb + 1, :], x_all[:, t - 1:t + 1, :]).then_inc(S["out_stored"], 16)
            sp.wait_ge(S["out_stored"], 16 * (T // 2))

        @block.gpsimd
        def _(pool):
            link = [0]

            def linked(ins):
                link[0] += 1
                ins.then_inc(S["pool_link"], 1)
                pool.wait_ge(S["pool_link"], link[0])

            pool.memset(kt_sb[:, :, :, :, :], 0.0).then_inc(S["blocks_cleared"], 1)
            pool.memset(ident[:, :], 0.0).then_inc(S["ident_cleared"], 1)
            pool.memset(zeros[:, :], 0.0).then_inc(S["zeros_set"], 1)
            pool.wait_ge(S["ident_cleared"], 1)
            pool.affine_select(out=ident[:, :], in_=ident[:, :], compare_op=ALU.not_equal, fill=1.0, base=0,
                               pattern=[[-1, P]], channel_multiplier=1).then_inc(S["ident_set"], 1)
            pool.memset(scratch[:, :], 0.0).then_inc(S["blocks_cleared"], 1)

            def bias(t):
                pool.wait_ge(S["xn1_set"], t + 1)
                pool.tensor_tensor(x_all[:, t, :], x_all[:, t, :], bo_sb[:, :], ALU.add).then_inc(S["x_biased"], 1)

            def newton(t, par):
                v, hv, y, w = (z[:, par:par + 1] for z in (var2, half2, rstd2, newton2))
                pool.wait_ge(S["guess2_set"], t + 1)
                for s in range(NEWTON):
                    pool.tensor_tensor(w, y, y, ALU.mult)
                    if s == 0:
                        pool.tensor_scalar(hv, v, -0.5, None, ALU.mult)
                    pool.drain()
                    pool.tensor_scalar(w, w, hv, 1.5, ALU.mult, ALU.add)
                    pool.drain()
                    last = pool.tensor_tensor(y, y, w, ALU.mult)
                    if s < NEWTON - 1:
                        pool.drain()
                last.then_inc(S["rstd2_set"], 1)

            def normalize(t, par):
                pool.wait_ge(S["recip_set"], t + 1)
                p3 = probs[:, par, :].rearrange("p (h m) -> p h m", h=H)
                pool.tensor_tensor(p3, p3, srec[:, par, :].unsqueeze(2).to_broadcast([P, H, M]),
                                   ALU.mult).then_inc(S["probs_set"], 1)

            pool.wait_ge(S["bo_in"], 16)
            for t in range(3):
                bias(t)
            normalize(0, 0)

            def step(t, par, static=False):
                if not static or t + 3 < T:
                    bias(t + 3)
                if not static or t >= 1:
                    newton(t - 1, 1 - par)
                if not static or t + 1 < T:
                    normalize(t + 1, 1 - par)

            for t in range(LOOP0):
                step(t, t % 2, True)
            tile_loop(pool, step)
            for t in range(LOOP1, T + 1):
                step(t, t % 2, True)

            linked(pool.iota(rank_first[:, :], pattern=[[-1, E]], base=E, channel_multiplier=0,
                             allow_small_or_imprecise_dtypes=True))
            pool.iota(step_rows[:, :], pattern=[[P, T]], base=0, channel_multiplier=0,
                      allow_small_or_imprecise_dtypes=True).then_inc(S["consts_set"], 1)
            pool.iota(tile_no[:, :], pattern=[[1, ET]], base=0, channel_multiplier=0,
                      allow_small_or_imprecise_dtypes=True).then_inc(S["consts_set"], 1)
            linked(pool.memset(before[:, :, :], 1.0))
            linked(pool.memset(earlier[:, :], 1.0))
            pool.memset(ones[:, :], 1.0).then_inc(S["consts_set"], 1)
            pool.affine_select(out=before[:, :, :], in_=before[:, :, :], compare_op=ALU.is_gt, fill=0.0, base=0,
                               pattern=[[1, E], [-1, E]], channel_multiplier=0).then_inc(S["consts_set"], 1)
            pool.affine_select(out=earlier[:, :], in_=earlier[:, :], compare_op=ALU.is_gt, fill=0.0, base=0,
                               pattern=[[1, P]], channel_multiplier=-1).then_inc(S["consts_set"], 1)

            for c in range(2):
                pool.wait_ge(xn2_saved[c], 16 * (T // 2))
            pool.wait_ge(S["zero_filled"], 16)
            pool.wait_ge(S["pos_set"], 1)
            for t in range(T):
                for c in range(2):
                    pool.indirect_dma_start(xs_dram, bass.IndirectOffsetOnAxis(pos[:, c, t:t + 1], 0),
                                            xn2_all[:, t, :], None).then_inc(S["scattered"], 16)

            pool.wait_ge(S["scattered"], 16 * 2 * T)
            for slot in range(RING):
                pool.wait_ge(ys_stored[slot], 16 * len(range(slot, ET, RING)))
            for t in range(T):
                for c, rows_of in enumerate((first, second)):
                    pool.indirect_dma_start(rows_of[:, t, :], None, ys_dram,
                                            bass.IndirectOffsetOnAxis(pos[:, c, t:t + 1], 0)).then_inc(gathered[t], 16)

        @block.tensor
        def _(pe):
            mm, transpose = nc.tensor.matmul, nc.tensor.transpose

            def kv_t(w, ps_of, ready):
                for j in range(PAIRS):
                    for k in range(KD):
                        last = mm(ps_of(j), w[:, k, j * P:(j + 1) * P], ctx_sb[:, k, :],
                                  start=(k == 0), stop=(k == KD - 1))
                    last.then_inc(ready, 1)

            def fold_q(n):
                b, k = n // KD, n % KD
                if n > KD:
                    pe.wait_ge(S["g_set_dve"], n)
                    pe.wait_ge(S["g_set_act"], n)
                if n == KD:
                    pe.wait_ge(S["vo_set"], KC)
                for j in range(PAIRS):
                    c = (j % 2) * 2 * M
                    last = mm(g_ps(n)[:, j // 2, c:c + 2 * M], wqt_sb[:, j, k * P:(k + 1) * P],
                              kt_sb[:, j, b, :, :].rearrange("p a m -> p (a m)"), start=True, stop=True)
                last.then_inc(S["g_in_ps"], 1)

            def fold_o(b):
                for c in range(KC):
                    n = b * KC + c
                    if n >= 2:
                        pe.wait_ge(S["vo_set"], n - 1)
                    pairs = [j for j in range(PAIRS) if j * 2 * M < c * P + KEYS[c] and (j + 1) * 2 * M > c * P]
                    for j in pairs:
                        last = mm(vo_ps(n)[0:KEYS[c], :], vt_sb[:, j, b, c * P:c * P + KEYS[c]],
                                  wo_sb[:, j, :], start=(j == pairs[0]), stop=(j == pairs[-1]))
                    last.then_inc(S["vo_in_ps"], 1)

            def turn_x(t, par, static=False):
                pe.wait_ge(S["xn1_set"], t + 1)
                if not static or t >= 3:
                    pe.wait_ge(S["pt_set_dve"], t - 2)
                if static and 1 <= t < 3:
                    pe.wait_ge(S["xt_set"], t)
                for k in range(KD):
                    last = transpose(turned[:, 1, (k + 1) * P:(k + 2) * P], xn1[:, par, k * P:(k + 1) * P], ident[:, :])
                last.then_inc(S["xt_in_ps"], 1)

            def scores(t, par, static=False):
                pe.wait_ge(S["xt_set"], t + 1)
                if not static or t >= 2:
                    pe.wait_ge(S["shifted"], t - 1)
                for half in range(2):
                    for k in range(KD):
                        last = mm(quad[:, par, half, 0:HALF], xt[:, par, k, :],
                                  g_sb[:, t // TB, k, half * HALF:(half + 1) * HALF],
                                  start=(k == 0), stop=(k == KD - 1))
                last.then_inc(S["scores_in_ps"], 1)

            def turn_probs(t, par, static=False):
                pe.wait_ge(S["probs_set"], t + 1)
                if not static or t >= 1:
                    pe.wait_ge(S["pt_set_act"], t)
                if not static or t + 2 < T:
                    pe.wait_ge(S["xt_set"], t + 3)
                for c in range(KC):
                    last = transpose(turned_flat[0:KEYS[c], c * P:(c + 1) * P], probs[:, par, c * P:c * P + KEYS[c]], ident[:, :])
                last.then_inc(S["pt_in_ps"], 1)

            def attend(t, par, static=False):
                pe.wait_ge(S["pt_set_act"], t + 1)
                pe.wait_ge(S["pt_set_dve"], t + 1)
                if not static or t >= 1:
                    pe.wait_ge(S["x2_set"], t)
                for c in range(KC):
                    last = mm(result_x, pt_sb[0:KEYS[c], c, :], vo_sb[0:KEYS[c], t // TB, c, :],
                              start=(c == 0), stop=(c == KC - 1))
                last.then_inc(S["attn_in_ps"], 1)

            def turn_xn2(t, par, static=False):
                pe.wait_ge(S["xn2_set"], t + 1)
                if not static or t >= 1:
                    pe.wait_ge(S["xn2t_set"], t)
                for k in range(KD):
                    last = transpose(result[:, 1, k * P:(k + 1) * P], xn2[:, par, k * P:(k + 1) * P], ident[:, :])
                last.then_inc(S["xn2t_in_ps"], 1)

            pe.wait_ge(S["kv_w_in"], 32)
            kv_t(wk_sb, lambda j: quad[:, j // 2, j % 2, 0:B * M], S["kt_in_ps"])
            pe.wait_ge(S["wv_in"], 16)
            kv_t(wv_sb, vt_ps, S["vt_in_ps"])
            pe.wait_ge(S["wq_in"], 16)
            pe.wait_ge(S["kt_set"], 2 * PAIRS)
            fold_q(0)
            pe.wait_ge(S["ident_set"], 1)
            pe.wait_ge(S["vt_set"], 2 * PAIRS)
            turn_x(0, 0, True)
            fold_q(1)
            turn_x(1, 1, True)
            pe.wait_ge(S["g_set_dve"], KD)
            pe.wait_ge(S["g_set_act"], KD)
            scores(0, 0, True)
            pe.wait_ge(S["wo_in"], 16)
            fold_o(0)
            fold_q(2)
            turn_x(2, 0, True)
            fold_q(3)
            pe.wait_ge(S["g_set_dve"], B * KD)
            fold_o(1)
            scores(1, 1, True)
            pe.wait_ge(S["g_set_dve"], B * KD)
            pe.wait_ge(S["g_set_act"], B * KD)
            pe.wait_ge(S["vo_set"], B * KC)

            def step(t, par, static=False):
                turn_probs(t, par, static)
                if not static or t + 2 < T:
                    scores(t + 2, par, static)
                if not static or t + 3 < T:
                    turn_x(t + 3, 1 - par, static)
                attend(t, par, static)
                if not static or t >= 1:
                    turn_xn2(t - 1, 1 - par, static)

            for t in range(LOOP0):
                step(t, t % 2, True)
            tile_loop(pe, step)
            for t in range(LOOP1, T):
                step(t, t % 2, True)
            turn_xn2(T - 1, 1, True)

            pe.wait_ge(S["wr_in"], 16)
            for g in range(T // G4):
                pe.wait_ge(S["xn2t_set"], G4 * (g + 1))
                if g == 0:
                    pe.wait_ge(S["shifted"], T)
                if g >= 2:
                    pe.wait_ge(S["lt_set"], g - 1)
                for k in range(KD):
                    last = mm(quad[0:NR, 0, g % 2, :], wr_sb[:, k, :], x2t_all[:, k, g * GT:(g + 1) * GT],
                              start=(k == 0), stop=(k == KD - 1))
                last.then_inc(S["lt_in_ps"], 1)
            for g in range(T // G4):
                pe.wait_ge(S["lt_set"], g + 1)
                for t in range(G4 * g, G4 * (g + 1)):
                    last = transpose(turned[:, 0, t * SCORE_W:t * SCORE_W + NR], lt_sb[:, t * P:(t + 1) * P], ident[0:NR, 0:NR])
            last.then_inc(S["logits_in_ps"], 1)

            def shared_in(g):
                for j in range(SJ):
                    n = g * SJ + j
                    if n >= 2:
                        pe.wait_ge(S["hs_set"], n - 1)
                    for half, ready in ((0, S["gate_in_ps"]), (1, S["up_in_ps"])):
                        for k in range(KD):
                            c = half * SHID + j * P
                            last = mm(quad[:, j % 2, half, :], wsi_sb[:, k, c:c + P], x2t_all[:, k, g * GT:(g + 1) * GT],
                                      start=(k == 0), stop=(k == KD - 1))
                        last.then_inc(ready, 1)

            def shared_out(g):
                pe.wait_ge(S["hs_set"], (g + 1) * SJ)
                for t in range(G4):
                    n = g * G4 + t
                    if n >= 2:
                        pe.wait_ge(S["shared_added"], n - 1)
                    for j in range(SJ):
                        last = mm(result[:, t % 2, 0:D], hs[:, g % 2, j, t * P:(t + 1) * P], wso_sb[:, j, :],
                                  start=(j == 0), stop=(j == SJ - 1))
                    last.then_inc(S["down_in_ps"], 1)

            pe.wait_ge(S["ws_in"], 32)
            shared_in(0)

            pe.wait_ge(S["consts_set"], 5)
            pe.wait_ge(S["picked_set"], 1)
            ranks = turned[:, 1, 0:T * E]
            mm(ranks, earlier[:, :], picked[:, :, :].rearrange("p t e -> p (t e)"), start=True, stop=False)
            for t in range(T - 1):
                later = T - 1 - t
                last = mm(turned[:, 1, (t + 1) * E:T * E].rearrange("p (t e) -> p t e", e=E), ones[:, :],
                          picked[:, t, :].unsqueeze(1).to_broadcast([P, later, E]), start=False, stop=(t == T - 2))
            last.then_inc(S["ranks_in_ps"], 1)
            pe.wait_ge(S["picked_t_set"], 1)
            mm(result[:, 1, 0:E], ones[:, :], picked_t[:, :], start=True, stop=True).then_inc(S["counts_in_ps"], 1)

            shared_in(1)
            shared_out(0)
            shared_out(1)

            def turn_xs(t, slot, par, load_no):
                pe.wait_ge(xs_in[slot], 16 * load_no)
                for k in range(KD):
                    last = transpose(turned[:, par, k * P:(k + 1) * P], xs[:, slot, k * P:(k + 1) * P], ident[:, :])
                last.then_inc(S["xst_in_ps"], 1)

            def expert_in(t, par):
                off = pe.value_load(expert_off[0:1, bass.ds(t, 1)], min_val=0, max_val=(E - 1) * EW)
                pe.wait_ge(S["xst_set"], t + 1)
                we = we_sb[:, :, :].rearrange("p e n -> p (e n)")
                for k in range(KD):
                    last = mm(quad[:, 0, par, 0:2 * P], xst[:, par, k, :], we[:, bass.ds(off + k * 2 * P, 2 * P)],
                              start=(k == 0), stop=(k == KD - 1))
                last.then_inc(S["gu_in_ps"], 1)

            def turn_h(t, par):
                pe.wait_ge(S["eh_set"], t + 1)
                transpose(quad[:, 1, par, 0:P], eh[:, par, :], ident[:, :]).then_inc(S["eht_in_ps"], 1)

            def expert_out(t, par, static=False):
                off = pe.value_load(expert_off[0:1, bass.ds(t, 1)], min_val=0, max_val=(E - 1) * EW)
                if not static or t >= 2:
                    pe.wait_ge(S["ys_set"], t - 1)
                pe.wait_ge(S["eht_set"], t + 1)
                we = we_sb[:, :, :].rearrange("p e n -> p (e n)")
                mm(result[:, par, 0:D], eht[:, par, :], we[:, bass.ds(off + KD * 2 * P, D)],
                   start=True, stop=True).then_inc(S["y_in_ps"], 1)

            pe.wait_ge(S["experts_set"], 1)
            pe.wait_ge(S["we_in"], 16)
            turn_xs(0, 0, 0, 1)
            turn_xs(1, 1, 1, 1)
            expert_in(0, 0)
            turn_xs(2, 2, 0, 1)
            expert_in(1, 1)
            pe.wait_ge(S["shared_added"], 2 * G4)

            def expert_step(t, c, i, static=False):
                turn_h(t, c % 2)
                if not static or t + 3 < ET:
                    turn_xs(t + 3, (c + 3) % RING, (c + 1) % 2, i + (c + 3) // RING + 1)
                if not static or t + 2 < ET:
                    expert_in(t + 2, c % 2)
                expert_out(t, c % 2, static)

            for t in range(RING):
                expert_step(t, t, 0, True)
            with pe.Fori(1, ELOOP // RING) as i:
                for c in range(RING):
                    expert_step(i * RING + c, c, i)
            for t in range(ELOOP, ET):
                expert_step(t, t % RING, t // RING, True)

            pe.wait_ge(S["ys_set"], ET)
            shared_in(2)
            shared_in(3)
            shared_out(2)
            shared_out(3)

        @block.scalar
        def _(act):
            copy = nc.scalar.copy
            x_rows = rows(x)
            for c in range(T // G4):
                b, tb = c * G4 // TB, c * G4 % TB
                act.dma_start(x_all[:, c * G4:(c + 1) * G4, :], x_rows[:, b, tb:tb + G4, :]).then_inc(x_in[c], 16)
            act.dma_start(bo_sb[:, :], bo.unsqueeze(0).to_broadcast([P, D])).then_inc(S["bo_in"], 16)

            act.wait_ge(S["blocks_cleared"], 2)
            for j in range(PAIRS):
                act.wait_ge(S["vt_in_ps"], j + 1)
                for a in range(2):
                    q = slice(a * P // 2, (a + 1) * P // 2)
                    at = (2 * j + a) * M
                    copy(vt_sb[q, j, :, at:at + M],
                         vt_ps(j)[q, :].rearrange("p (b m) -> p b m", b=B)).then_inc(S["vt_set"], 1)

            def g_out(n):
                act.wait_ge(S["g_in_ps"], n + 1)
                copy(g_sb[:, n // KD, n % KD, HALF:HM], g_ps(n)[:, 1, 0:HALF]).then_inc(S["g_set_act"], 1)

            def xt_out(t, par, static=False):
                act.wait_ge(S["xt_in_ps"], t + 1)
                if not static or t >= 2:
                    act.wait_ge(S["scores_in_ps"], t - 1)
                copy(xt[:, par, :, :].rearrange("p k c -> p (k c)"), turned[:, 1, P:P + D]).then_inc(S["xt_set"], 1)

            def vo_out(n):
                act.wait_ge(S["vo_in_ps"], n + 1)
                b, c = n // KC, n % KC
                copy(vo_sb[0:KEYS[c], b, c, :], vo_ps(n)[0:KEYS[c], :]).then_inc(S["vo_set"], 1)

            def exps(t, par, static=False):
                act.wait_ge(S["shifted"], t + 1)
                nc.scalar.activation(probs[:, par, :], probs[:, par, :], ACT.Exp, scale=SCALE).then_inc(S["exps_set"], 1)

            g_out(0)
            xt_out(0, 0, True)
            g_out(1)
            xt_out(1, 1, True)
            for c in range(KC):
                vo_out(c)
            g_out(2)
            xt_out(2, 0, True)
            g_out(3)
            exps(0, 0)
            for c in range(KC):
                vo_out(KC + c)

            def pt_out(t):
                act.wait_ge(S["pt_in_ps"], t + 1)
                copy(pt_sb[:, 0:KC - 1, :].rearrange("p c k -> p (c k)"), turned[:, 0, :]).then_inc(S["pt_set_act"], 1)

            def xn2t_out(t):
                act.wait_ge(S["xn2t_in_ps"], t + 1)
                copy(x2t_all[:, :, bass.ds(t * P, P)],
                     result[:, 1, 0:KD * P].rearrange("p (k c) -> p k c", k=KD)).then_inc(S["xn2t_set"], 1)

            def step(t, par, static=False):
                pt_out(t)
                if not static or t + 1 < T:
                    exps(t + 1, 1 - par)
                if not static or t + 3 < T:
                    xt_out(t + 3, 1 - par, static)
                if not static or t >= 1:
                    xn2t_out(t - 1)

            for t in range(LOOP0):
                step(t, t % 2, True)
            tile_loop(act, step)
            for t in range(LOOP1, T):
                step(t, t % 2, True)
            xn2t_out(T - 1)

            for g in range(T // G4):
                act.wait_ge(S["lt_in_ps"], g + 1)
                copy(lt_sb[:, g * GT:(g + 1) * GT], quad[0:NR, 0, g % 2, :]).then_inc(S["lt_set"], 1)

            def shared_tanh(n):
                act.wait_ge(S["gate_in_ps"], n + 1)
                if n >= 2:
                    act.wait_ge(S["ga_set"], n - 1)
                nc.scalar.activation(th[:, n % 2, :], quad[:, n % 2, 0, :], ACT.Tanh, scale=0.5).then_inc(S["tanh_set"], 1)

            shared_tanh(0)
            act.wait_ge(S["gaps_set"], 1)
            nc.scalar.activation(tgate[:, :], lg[:, :, E], ACT.Tanh, scale=0.5).then_inc(S["tgate_set"], 1)
            nc.scalar.activation(egap[:, :], gap[:, :], ACT.Exp).then_inc(S["egap_set"], 1)
            for n in range(1, 2 * SJ):
                shared_tanh(n)

            def xst_out(t, par, static=False):
                act.wait_ge(S["xst_in_ps"], t + 1)
                if not static or t >= 2:
                    act.wait_ge(S["gu_in_ps"], t - 1)
                copy(xst[:, par, :, :].rearrange("p k c -> p (k c)"), turned[:, par, 0:D]).then_inc(S["xst_set"], 1)

            def expert_tanh(t, par, static=False):
                act.wait_ge(S["gu_in_ps"], t + 1)
                if not static or t >= 2:
                    act.wait_ge(S["ega_set"], t - 1)
                nc.scalar.activation(eth[:, par, :], quad[:, 0, par, 0:P], ACT.Tanh,
                                     scale=0.5).then_inc(S["eth_set"], 1)

            def y_out(t, c, i, static=False):
                act.wait_ge(S["y_in_ps"], t + 1)
                if not static or t >= RING:
                    act.wait_ge(ys_stored[c], 16 * i)
                copy(ys[:, c, :], result[:, c % 2, 0:D]).then_inc(S["ys_set"], 1)

            xst_out(0, 0, True)
            xst_out(1, 1, True)
            expert_tanh(0, 0, True)
            xst_out(2, 0, True)
            expert_tanh(1, 1, True)

            def expert_step(t, c, i, static=False):
                if not static or t + 3 < ET:
                    xst_out(t + 3, (c + 1) % 2)
                if not static or t + 2 < ET:
                    expert_tanh(t + 2, c % 2)
                y_out(t, c, i, static)

            for t in range(RING):
                expert_step(t, t, 0, True)
            with act.Fori(1, ELOOP // RING) as i:
                for c in range(RING):
                    expert_step(i * RING + c, c, i)
            for t in range(ELOOP, ET):
                expert_step(t, t % RING, t // RING, True)

            for n in range(2 * SJ, 4 * SJ):
                shared_tanh(n)

        @block.vector
        def _(dve):
            v = nc.vector
            link = [0]

            def linked(ins):
                link[0] += 1
                ins.then_inc(S["dve_link"], 1)
                dve.wait_ge(S["dve_link"], link[0])

            dve.wait_ge(S["blocks_cleared"], 1)
            for j in range(PAIRS):
                dve.wait_ge(S["kt_in_ps"], j + 1)
                for a in range(2):
                    q = slice(a * P // 2, (a + 1) * P // 2)
                    v.tensor_copy(kt_sb[q, j, :, a, :],
                                  quad[q, j // 2, j % 2, 0:B * M].rearrange("p (b m) -> p b m", b=B)).then_inc(S["kt_set"], 1)

            def norm1(t0, t1):
                for t in range(t0, t1):
                    if t % G4 == 0:
                        dve.wait_ge(x_in[t // G4], 16)
                    ins = v.bn_stats(stats[:, t, :], x_all[:, t, :])
                linked(ins)
                for t in range(t0, t1):
                    ins = v.bn_aggr(moments1[:, t, :], stats[:, t, :])
                linked(ins)
                va, y, w = (z[:, t0:t1] for z in (var1, rstd1, newton1))
                linked(v.tensor_scalar(va, moments1[:, t0:t1, 1], LN_EPS, None, ALU.add))
                linked(v.tensor_scalar(w.bitcast(I32), va.bitcast(I32), 1, None, ALU.logical_shift_right))
                linked(v.tensor_scalar(y.bitcast(I32), w.bitcast(I32), -1.0, float(RSQRT_MAGIC), ALU.mult, ALU.add))
                for _ in range(NEWTON):
                    linked(v.tensor_tensor(w, y, y, ALU.mult))
                    linked(v.scalar_tensor_tensor(w, w, -0.5, va, ALU.mult, ALU.mult))
                    linked(v.scalar_tensor_tensor(y, w, 1.5, y, ALU.add, ALU.mult))

            def apply1(t, par, static=False):
                if not static or t >= 2:
                    dve.wait_ge(S["xt_in_ps"], t - 1)
                tt = bass.ds(t, 1)
                v.tensor_scalar(xn1[:, par, :], x_all[:, t, :], moments1[:, t, 0:1], rstd1[:, tt],
                                ALU.subtract, ALU.mult).then_inc(S["xn1_set"], 1)

            def g_out(n):
                dve.wait_ge(S["g_in_ps"], n + 1)
                v.tensor_copy(g_sb[:, n // KD, n % KD, 0:HALF], g_ps(n)[:, 0, 0:HALF]).then_inc(S["g_set_dve"], 1)

            def shift(t, par, static=False):
                s4 = quad[:, par, :, 0:HALF].rearrange("p a (h m) -> p a h m", h=HH)
                mx = smax[:, par, :].rearrange("p (a h) -> p a h", a=2)
                dve.wait_ge(S["scores_in_ps"], t + 1)
                v.tensor_reduce(mx, s4, AX, ALU.max).then_inc(S["max_found"], 1)
                dve.wait_ge(S["max_found"], t + 1)
                if not static or t >= 2:
                    dve.wait_ge(S["pt_in_ps"], t - 1)
                v.tensor_tensor(probs[:, par, :].rearrange("p (a h m) -> p a h m", a=2, h=HH), s4,
                                mx.unsqueeze(3).to_broadcast([P, 2, HH, M]), ALU.subtract).then_inc(S["shifted"], 1)

            def sums(t, par, static=False):
                dve.wait_ge(S["exps_set"], t + 1)
                v.tensor_reduce(ssum[:, par, :], probs[:, par, :].rearrange("p (h m) -> p h m", h=H), AX,
                                ALU.add).then_inc(S["summed"], 1)
                dve.wait_ge(S["summed"], t + 1)
                v.reciprocal(srec[:, par, :], ssum[:, par, :]).then_inc(S["recip_set"], 1)

            norm1(0, G4)
            apply1(0, 0, True)
            apply1(1, 1, True)
            g_out(0)
            g_out(1)
            apply1(2, 0, True)
            shift(0, 0, True)
            g_out(2)
            sums(0, 0, True)
            g_out(3)
            norm1(G4, T)

            def pt_out(t):
                dve.wait_ge(S["pt_in_ps"], t + 1)
                v.tensor_copy(pt_sb[0:KEYS[-1], KC - 1, :], turned[0:KEYS[-1], 1, 0:P]).then_inc(S["pt_set_dve"], 1)

            def residual(t, par):
                dve.wait_ge(S["attn_in_ps"], t + 1)
                dve.wait_ge(S["x_biased"], t + 1)
                v.tensor_tensor(x_all[:, t, :], result_x, x_all[:, t, :], ALU.add).then_inc(S["x2_set"], 1)
                apart(dve)
                dve.wait_ge(S["x2_set"], t + 1)
                v.bn_stats(stats2[:, :], x_all[:, t, :]).then_inc(S["stats2_set"], 1)
                apart(dve)
                dve.wait_ge(S["stats2_set"], t + 1)
                v.bn_aggr(moments2[:, par, :], stats2[:, :]).then_inc(S["moments2_set"], 1)
                va, y, w = (z[:, par:par + 1] for z in (var2, rstd2, newton2))
                dve.wait_ge(S["moments2_set"], t + 1)
                v.tensor_scalar(va, moments2[:, par, 1:2], LN_EPS, None, ALU.add).then_inc(S["var2_set"], 1)
                dve.wait_ge(S["var2_set"], 2 * t + 1)
                v.tensor_scalar(w.bitcast(I32), va.bitcast(I32), 1, None, ALU.logical_shift_right).then_inc(S["var2_set"], 1)
                dve.wait_ge(S["var2_set"], 2 * t + 2)
                v.tensor_scalar(y.bitcast(I32), w.bitcast(I32), -1.0, float(RSQRT_MAGIC), ALU.mult,
                                ALU.add).then_inc(S["guess2_set"], 1)

            def apply2(t, par, static=False):
                dve.wait_ge(S["rstd2_set"], t + 1)
                if not static or t >= 2:
                    dve.wait_ge(S["xn2t_in_ps"], t - 1)
                    dve.wait_ge(xn2_saved[par], 8 * (t - par))
                v.tensor_scalar(xn2[:, par, :], x_all[:, t, :], moments2[:, par, 0:1], rstd2[:, par:par + 1],
                                ALU.subtract, ALU.mult).then_inc(S["xn2_set"], 1)

            def step(t, par, static=False):
                if not static or t + 1 < T:
                    shift(t + 1, 1 - par, static)
                if not static or t < T:
                    pt_out(t)
                if not static or t + 3 < T:
                    apply1(t + 3, 1 - par, static)
                if not static or t >= 1:
                    residual(t - 1, 1 - par)
                if not static or t + 1 < T:
                    sums(t + 1, 1 - par, static)
                if not static or t >= 1:
                    apply2(t - 1, 1 - par, static)

            for t in range(LOOP0):
                step(t, t % 2, True)
            tile_loop(dve, step)
            for t in range(LOOP1, T + 1):
                step(t, t % 2, True)

            def te(z):
                return z.unsqueeze(2).to_broadcast([P, T, E])

            first_rank = rank_first[:, :].unsqueeze(1).to_broadcast([P, T, E])
            dve.wait_ge(S["logits_in_ps"], 1)
            linked(v.tensor_copy(lg[:, :, :], turned[:, 0, 0:T * SCORE_W].rearrange("p (t n) -> p t n", n=SCORE_W)[:, :, 0:NR]))
            dve.wait_ge(S["consts_set"], 5)

            def choose(l, top, oh):
                linked(v.tensor_reduce(top, l, AX, ALU.max))
                linked(v.tensor_tensor(eq[:, :, :], l, te(top), ALU.is_equal))
                linked(v.tensor_tensor(eq[:, :, :], eq[:, :, :], first_rank, ALU.mult))
                linked(v.tensor_reduce(pick[:, :], eq[:, :, :], AX, ALU.max))
                linked(v.tensor_tensor(oh, eq[:, :, :], te(pick[:, :]), ALU.is_equal))

            choose(lg[:, :, 0:E], top1[:, :], oh1[:, :, :])
            linked(v.scalar_tensor_tensor(lg2[:, :, :], oh1[:, :, :], MASKED, lg[:, :, 0:E], ALU.mult, ALU.add))
            choose(lg2[:, :, :], top2[:, :], oh2[:, :, :])
            v.tensor_tensor(gap[:, :], top2[:, :], top1[:, :], ALU.subtract).then_inc(S["gaps_set"], 1)
            v.tensor_tensor(picked[:, :, :], oh1[:, :, :], oh2[:, :, :], ALU.add).then_inc(S["picked_set"], 1)
            dve.wait_ge(S["picked_set"], 1)
            with nc.allow_low_precision(reason="counts up to 16 are exact in bfloat16"):
                v.tensor_reduce(picked_t[:, :], picked[:, :, :].rearrange("p t e -> p e t"), AX, ALU.add).then_inc(S["picked_t_set"], 1)

            def shared_h(n):
                g, j = n // SJ, n % SJ
                dve.wait_ge(S["tanh_set"], n + 1)
                v.scalar_tensor_tensor(ga[:, n % 2, :], th[:, n % 2, :], 1.0, quad[:, j % 2, 0, :], ALU.add,
                                       ALU.mult).then_inc(S["ga_set"], 1)
                dve.wait_ge(S["ga_set"], n + 1)
                dve.wait_ge(S["up_in_ps"], n + 1)
                if g >= 2:
                    dve.wait_ge(S["down_in_ps"], (g - 1) * G4)
                v.tensor_tensor(hs[:, g % 2, j, :], ga[:, n % 2, :], quad[:, j % 2, 1, :], ALU.mult).then_inc(S["hs_set"], 1)

            for n in range(2):
                shared_h(n)

            dve.wait_ge(S["counts_in_ps"], 1)
            linked(v.tensor_copy(counts[:, :], result[:, 1, 0:E]))
            linked(v.tensor_tensor(eq[:, 0:E, :], counts[:, :].unsqueeze(2).to_broadcast([P, E, T]),
                                   step_rows[:, :].unsqueeze(1).to_broadcast([P, E, T]), ALU.is_gt))
            linked(v.tensor_reduce(ntiles[:, :], eq[:, 0:E, :], AX, ALU.add))
            linked(v.tensor_tensor(lg2[:, 0:E, :], before[:, :, :], ntiles[:, :].unsqueeze(1).to_broadcast([P, E, E]), ALU.mult))
            linked(v.tensor_reduce(base[:, :], lg2[:, 0:E, :], AX, ALU.add))
            linked(v.tensor_scalar(base_row[:, :], base[:, :], float(P), None, ALU.mult))
            linked(v.tensor_tensor(lg2[:, :, :], turned[:, 1, 0:T * E].rearrange("p (t e) -> p t e", e=E),
                                   base_row[:, :].unsqueeze(1).to_broadcast([P, T, E]), ALU.add))
            for c, oh in enumerate((oh1, oh2)):
                linked(v.tensor_tensor(eq[:, :, :], oh[:, :, :], lg2[:, :, :], ALU.mult))
                linked(v.tensor_reduce(posf[:, c, :], eq[:, :, :], AX, ALU.add))
            v.tensor_copy(pos[:, :, :], posf[:, :, :]).then_inc(S["pos_set"], 1)
            linked(v.tensor_tensor(base_end[:, :], base[:, :], ntiles[:, :], ALU.add))
            linked(v.tensor_tensor(past[:, :, :], base_end[0:1, :].unsqueeze(1).to_broadcast([1, ET, E]),
                                   tile_no[:, :].unsqueeze(2).to_broadcast([1, ET, E]), ALU.is_le))
            linked(v.tensor_reduce(ewf[:, :], past[:, :, :], AX, ALU.add))
            linked(v.tensor_scalar(ewf[:, :], ewf[:, :], float(E - 1), float(EW), ALU.min, ALU.mult))
            v.tensor_copy(expert_off[:, :], ewf[:, :]).then_inc(S["experts_set"], 1)
            dve.wait_ge(S["egap_set"], 1)
            linked(v.tensor_scalar(gap[:, :], egap[:, :], 2.0, 2.0, ALU.mult, ALU.add))
            linked(v.reciprocal(w12[:, 0, :], gap[:, :]))
            linked(v.tensor_tensor(w12[:, 1, :], w12[:, 0, :], egap[:, :], ALU.mult))
            dve.wait_ge(S["tgate_set"], 1)
            linked(v.tensor_scalar(sgate[:, :], tgate[:, :], 0.25, 0.25, ALU.mult, ALU.add))

            for n in range(2, 2 * SJ):
                shared_h(n)

            def add_shared(t):
                dve.wait_ge(S["down_in_ps"], t + 1)
                v.scalar_tensor_tensor(x_all[:, t, :], result[:, t % 2, 0:D], sgate[:, t:t + 1],
                                       x_all[:, t, :], ALU.mult, ALU.add).then_inc(S["shared_added"], 1)

            for t in range(2 * G4):
                add_shared(t)

            def expert_h(t, par, static=False):
                dve.wait_ge(S["eth_set"], t + 1)
                v.scalar_tensor_tensor(ega[:, par, :], eth[:, par, :], 1.0, quad[:, 0, par, 0:P], ALU.add,
                                       ALU.mult).then_inc(S["ega_set"], 1)
                dve.wait_ge(S["ega_set"], t + 1)
                if not static or t >= 2:
                    dve.wait_ge(S["eht_in_ps"], t - 1)
                v.tensor_tensor(eh[:, par, :], ega[:, par, :], quad[:, 0, par, P:2 * P], ALU.mult).then_inc(S["eh_set"], 1)

            def eht_out(t, par, static=False):
                dve.wait_ge(S["eht_in_ps"], t + 1)
                if not static or t >= 2:
                    dve.wait_ge(S["y_in_ps"], t - 1)
                v.tensor_copy(eht[:, par, :], quad[:, 1, par, 0:P]).then_inc(S["eht_set"], 1)

            expert_h(0, 0, True)
            expert_h(1, 1, True)

            def expert_step(t, c, i, static=False):
                eht_out(t, c % 2, static)
                if not static or t + 2 < ET:
                    expert_h(t + 2, c % 2)

            for t in range(RING):
                expert_step(t, t, 0, True)
            with dve.Fori(1, ELOOP // RING) as i:
                for c in range(RING):
                    expert_step(i * RING + c, c, i)
            for t in range(ELOOP, ET):
                expert_step(t, t % RING, t // RING, True)

            def combine(t):
                dve.wait_ge(gathered[t], 32)
                dve.wait_ge(S["shared_added"], t + 1)
                v.scalar_tensor_tensor(x_all[:, t, :], first[:, t, :], w12[:, 0, t:t + 1], x_all[:, t, :],
                                       ALU.mult, ALU.add).then_inc(S["first_added"], 1)
                dve.wait_ge(S["first_added"], t + 1)
                v.scalar_tensor_tensor(x_all[:, t, :], second[:, t, :], w12[:, 1, t:t + 1], x_all[:, t, :],
                                       ALU.mult, ALU.add).then_inc(S["combined"], 1)

            for n in range(2 * SJ, 3 * SJ):
                shared_h(n)
            for n in range(3 * SJ, 4 * SJ):
                shared_h(n)
            for t in range(2 * G4):
                combine(t)
            for t in range(2 * G4, T):
                add_shared(t)
                combine(t)


def kernel(**inputs):
    import numpy as np
    import concourse.bacc as bacc
    from concourse.bass_utils import run_bass_kernel_spmd

    a = {k: np.asarray(v) for k, v in inputs.items()}
    x, c = a["x"], a["ctx_1024"]
    B, N, D = x.shape
    M = c.shape[1]
    gate, up, down = a["L0_ffn_We_gate"], a["L0_ffn_We_up"], a["L0_ffn_We_down"]
    E, HID, _ = gate.shape
    KD = D // P
    gu = np.concatenate([gate, up], axis=1).transpose(0, 2, 1).reshape(E, KD, P, 2 * HID)
    w_expert = np.concatenate([gu[:, k] for k in range(KD)] + [down.transpose(0, 2, 1)], axis=2)
    arrays = {
        "x": x,
        "ctx_t": c.transpose(2, 0, 1).reshape(D, B * M),
        "wk": a["L0_xattn_Wk"],
        "wv": a["L0_xattn_Wv"],
        "wq_t": a["L0_xattn_Wq"].T,
        "wo": a["L0_xattn_Wo"],
        "bo": a["L0_xattn_bo"],
        "w_router": np.concatenate([a["L0_ffn_Wg"], a["L0_ffn_Wsg"]], axis=0).T,
        "w_expert": w_expert,
        "w_shared_in": np.concatenate([a["L0_ffn_Ws_gate"], a["L0_ffn_Ws_up"]], axis=0).T,
        "w_shared_out": a["L0_ffn_Ws_down"].T,
    }
    nc = bacc.Bacc("TRN2", target_bir_lowering=False, num_devices=1)
    named, args = {}, []
    for name, v in arrays.items():
        v = np.ascontiguousarray(v)
        named[f"in_{name}"] = v
        args.append(nc.dram_tensor(f"in_{name}", v.shape, mybir.dt.from_np(v.dtype), kind="ExternalInput").ap())
    args.append(nc.dram_tensor("out_x", (B, N, D), F32, kind="ExternalOutput").ap())
    build(nc, *args)
    r = run_bass_kernel_spmd(nc, [named], core_ids=[0])
    return r.results[0]["out_x"]
```

```python
from contextlib import ExitStack

import concourse.bass as bass
from concourse import mybir

ALU = mybir.AluOpType
ACT = mybir.ActivationFunctionType
AX = mybir.AxisListType.X
F32 = mybir.dt.float32
BF16 = mybir.dt.bfloat16
I32 = mybir.dt.int32
U32 = mybir.dt.uint32

P = 128
BANK = 512
XS_RING = 8
YS_RING = 4
LN_EPS = 1e-5
RSQRT_MAGIC = 0x5F3759DF
NEWTON = 3
MASKED = -3.0e38


def build(nc, x, ctx_t, wk, wv, wq_t, wo, bo, w_router, w_expert, w_shared_in, w_shared_out, out):
    B, N, D = x.shape
    KD = D // P
    INNER = wk.shape[1]
    PAIRS = INNER // P
    M = ctx_t.shape[1] // B
    H = 2 * PAIRS
    HM = H * M
    HALF = HM // 2
    HH = H // 2
    KEYS = [min(P, HM - c) for c in range(0, HM, P)]
    KC = len(KEYS)
    SCALE = float(INNER // H) ** -0.5
    TB = N // P
    T = B * TB
    E = w_expert.shape[0]
    EW = w_expert.shape[2]
    NR = w_router.shape[1]
    SJ = w_shared_out.shape[0] // P
    SHID = SJ * P
    G4 = 4
    GT = G4 * P
    ET = 2 * T + E - 1
    SCORE_W = NR + 1

    XW = D + 4
    xs_dram = nc.dram_tensor("tokens_by_expert", (ET * P, XW), F32, kind="Internal").ap()
    results_dram = nc.dram_tensor("results", ((2 * T + ET) * P, D), F32, kind="Internal").ap()

    with ExitStack() as ctx:
        def sb(name, shape, dt=F32):
            return ctx.enter_context(nc.sbuf_tensor(name, shape, dt))

        def psum(name, shape):
            return ctx.enter_context(nc.psum_tensor(name, shape, F32))

        def sem(name):
            return ctx.enter_context(nc.semaphore(name))

        x_all = sb("x_all", [P, T, D])
        xn2_all = sb("xn2_all", [P, T, XW])
        x2t_all = sb("x2t_all", [P, KD, T * P])
        scratch = sb("scratch", [P, PAIRS * B * KC * P])
        ctx_sb = sb("ctx_sb", [P, KD, B * M])
        attn_w = sb("attn_w", [P, 4, KD * INNER])
        bo_sb = sb("bo_sb", [1, D])
        head0 = sb("head0", [1, P])
        kt_sb = sb("kt_sb", [P, PAIRS, B, 2, M])
        folded = sb("folded", [P, B * KD * HM + B * KC * D])
        wr_sb = sb("wr_sb", [P, KD, NR])
        we_sb = sb("we_sb", [P, E, EW])
        wsi_sb = sb("wsi_sb", [P, KD, 2 * SHID])
        wso_sb = sb("wso_sb", [P, SJ, D])
        ident = sb("ident", [P, P])
        filler = sb("filler", [P, D])
        stats = sb("stats", [P, T, 6])
        moments1 = sb("moments1", [P, T, 2])
        var1 = sb("var1", [P, T])
        rstd1 = sb("rstd1", [P, T])
        newton1 = sb("newton1", [P, T])
        stats2 = sb("stats2", [P, 6])
        moments2 = sb("moments2", [P, 2, 2])
        var2 = sb("var2", [P, 2])
        half2 = sb("half2", [P, 2])
        rstd2 = sb("rstd2", [P, 2])
        newton2 = sb("newton2", [P, 2])
        xn1 = sb("xn1", [P, 2, D])
        xt = sb("xt", [P, 2, KD, P])
        xn2 = sb("xn2", [P, 2, D])
        smax = sb("smax", [P, 2, H])
        ssum = sb("ssum", [P, 2, H])
        srec = sb("srec", [P, 2, H])
        probs = sb("probs", [P, 2, HM])
        pt_sb = sb("pt_sb", [P, KC, P])
        th = sb("th", [P, 2, GT])
        ga = sb("ga", [P, 2, GT])
        lg = sb("lg", [P, T, NR])
        lg2 = sb("lg2", [P, T, E])
        eq = sb("eq", [P, T, E])
        oh1 = sb("oh1", [P, T, E])
        oh2 = sb("oh2", [P, T, E])
        top1 = sb("top1", [P, T])
        top2 = sb("top2", [P, T])
        pick = sb("pick", [P, T])
        picked = sb("picked", [P, T, E], BF16)
        picked_t = sb("picked_t", [P, E], BF16)
        earlier = sb("earlier", [P, P], BF16)
        ones = sb("ones", [P, P], BF16)
        rank_first = sb("rank_first", [P, E])
        result_row = sb("result_row", [P, T], I32)
        step_rows = sb("step_rows", [P, T])
        before = sb("before", [P, E, E])
        tile_no = sb("tile_no", [1, ET])
        counts = sb("counts", [P, E])
        ntiles = sb("ntiles", [P, E])
        base = sb("base", [P, E])
        base_end = sb("base_end", [P, E])
        base_row = sb("base_row", [P, E])
        past = sb("past", [1, ET, E])
        ewf = sb("ewf", [1, ET])
        expert_off = sb("expert_off", [1, ET], I32)
        posf = sb("posf", [P, 2, T])
        pos = sb("pos", [P, 2, T], U32)
        w12 = sb("w12", [P, 2, T])
        gap = sb("gap", [P, T])
        egap = sb("egap", [P, T])
        tgate = sb("tgate", [P, T])
        sgate = sb("sgate", [P, T])

        quad = psum("quad", [P, 2, 2, BANK])
        turned = psum("turned", [P, 2, BANK])
        result = psum("result", [P, 2, BANK])
        turned_flat = turned[:, :, :].rearrange("p a n -> p (a n)")
        result_x = result[:, 0, 0:D]

        vt_sb = scratch[:, :].rearrange("p (j b c) -> p j b c", j=PAIRS, b=B)
        second = scratch[:, 0:T * D].rearrange("p (t d) -> p t d", t=T)
        g_sb = folded[:, 0:B * KD * HM].rearrange("p (b k n) -> p b k n", b=B, k=KD)
        vo_sb = folded[:, B * KD * HM:].rearrange("p (b c n) -> p b c n", b=B, c=KC)
        at = [0]

        def part(n, size):
            view = folded[:, at[0]:at[0] + n * size].rearrange("p (n c) -> p n c", n=n)
            at[0] += n * size
            return view

        xs, ys = part(XS_RING, XW), part(YS_RING, D)
        xst = part(2, KD * P).rearrange("p n (k c) -> p n k c", k=KD)
        eth, ega, eh, eht = part(2, P), part(2, P), part(2, P), part(2, P)
        first = xn2_all[:, :, 0:D]
        spare = th[:, 0, 0:ET * (XW - D)].rearrange("p (t c) -> p t c", t=ET)
        lt_sb = scratch[0:NR, 0:T * P]
        wk_sb = attn_w[:, 0, :].rearrange("p (k n) -> p k n", k=KD)
        wv_sb = attn_w[:, 1, :].rearrange("p (k n) -> p k n", k=KD)
        wqt_sb = attn_w[:, 2, :].rearrange("p (j n) -> p j n", j=PAIRS)
        wo_sb = attn_w[:, 3, :].rearrange("p (j n) -> p j n", j=PAIRS)
        hs = attn_w[:, :, :].rearrange("p a (b n) -> p (a b) n", n=GT).rearrange("p (g j) n -> p g j n", g=2)

        names = """kv_w_in wv_in wq_in wo_in bo_in wr_in ws_in we_in rows_filled filler_set blocks_cleared
            ident_cleared ident_set kt_in_ps kt_set vt_in_ps vt_set g_in_ps g_set_dve g_set_act vo_in_ps vo_set
            dve_link pool_link consts_set
            xn1_set xt_in_ps xt_set scores_in_ps max_found shifted exps_set summed recip_set probs_set
            pt_in_ps pt_set_act pt_set_dve attn_in_ps x2_set stats2_set moments2_set var2_set guess2_set
            rstd2_set xn2_set xn2t_in_ps xn2t_set
            lt_in_ps lt_set logits_in_ps picked_set picked_t_set ranks_in_ps counts_in_ps gaps_set egap_set tgate_set
            pos_set experts_set weights_set scattered first_sent rows_set head0_set
            gate_in_ps up_in_ps tanh_set ga_set hs_set down_in_ps shared_added
            xst_in_ps xst_set gu_in_ps eth_set ega_set eh_set eht_in_ps eht_set y_in_ps ys_set
            choices_added first_added combined out_stored""".split()
        S = {n: sem(n) for n in names}
        x_in = [sem(f"x_in{c}") for c in range(T // G4)]
        xn2_saved = [sem(f"xn2_saved{c}") for c in range(2)]
        xs_in = [sem(f"xs_in{c}") for c in range(XS_RING)]
        ys_sent = [sem(f"ys_sent{c}") for c in range(YS_RING)]
        results_in = [sem(f"results_in{q}") for q in range(T // G4)]

        def g_ps(n):
            return quad[:, n, :, :] if n < KD else result[:, :, :]

        def vt_ps(j):
            return (turned if j < 2 else result)[:, j % 2, 0:B * M]

        def vo_ps(n):
            return (turned if n % 2 else result)[:, 0, 0:D]

        def rows(ap):
            return ap.rearrange("b (p t) d -> p b t d", p=P)

        LOOP0, LOOP1 = 4, T - 4

        def tile_loop(eng, body):
            with eng.Fori(0, (LOOP1 - LOOP0) // 2) as i:
                for c in range(2):
                    body(i * 2 + (LOOP0 + c), c)

        ELOOP = (ET - 3) // XS_RING * XS_RING

        def expert_steps(eng, step):
            for t in range(XS_RING):
                step(t, t, 0, t // YS_RING, True)
            with eng.Fori(1, ELOOP // XS_RING) as i:
                for c in range(XS_RING):
                    step(i * XS_RING + c, c, i, i * (XS_RING // YS_RING) + c // YS_RING, False)
            for t in range(ELOOP, ET):
                step(t, t % XS_RING, t // XS_RING, t // YS_RING, True)

        def apart(eng):
            eng.wait_ge(S["filler_set"], 1)

        block = ctx.enter_context(nc.Block())

        @block.sync
        def _(sp):
            sp.dma_start(ctx_sb[:, :, :], ctx_t.rearrange("(k p) m -> p k m", p=P)).then_inc(S["kv_w_in"], 16)
            sp.dma_start(wk_sb[:, :, :], wk.rearrange("(k p) n -> p k n", p=P)).then_inc(S["kv_w_in"], 16)
            sp.dma_start(wqt_sb[:, :, :], wq_t.rearrange("(j p) n -> p j n", p=P)).then_inc(S["wq_in"], 16)
            sp.dma_start(wv_sb[:, :, :], wv.rearrange("(k p) n -> p k n", p=P)).then_inc(S["wv_in"], 16)
            sp.dma_start(wo_sb[:, :, :], wo.rearrange("(j p) n -> p j n", p=P)).then_inc(S["wo_in"], 16)
            for c in range(1, T // G4):
                b, tb = c * G4 // TB, c * G4 % TB
                sp.dma_start(x_all[:, c * G4:(c + 1) * G4, :], rows(x)[:, b, tb:tb + G4, :]).then_inc(x_in[c], 16)
            sp.dma_start(wr_sb[:, :, :], w_router.rearrange("(k p) n -> p k n", p=P)).then_inc(S["wr_in"], 16)
            sp.dma_start(wsi_sb[:, :, :], w_shared_in.rearrange("(k p) n -> p k n", p=P)).then_inc(S["ws_in"], 16)
            sp.dma_start(wso_sb[:, :, :], w_shared_out.rearrange("(j p) n -> p j n", p=P)).then_inc(S["ws_in"], 16)
            sp.wait_ge(S["filler_set"], 2)
            xs_rows = xs_dram.rearrange("(r p) d -> p r d", p=P)
            sp.dma_start(xs_rows[:, :, 0:D], filler[:, :].unsqueeze(1).to_broadcast([P, ET, D])).then_inc(S["rows_filled"], 16)
            sp.dma_start(xs_rows[:, :, D:XW], spare[:, :, :]).then_inc(S["rows_filled"], 16)
            sp.dma_start(we_sb[:, :, :], w_expert.rearrange("e p n -> p e n")).then_inc(S["we_in"], 16)

            def save(t, par):
                sp.wait_ge(S["xn2_set"], t + 1)
                sp.dma_start(xn2_all[:, t, 0:D], xn2[:, par, :]).then_inc(xn2_saved[par], 16)

            for t in range(LOOP0):
                save(t, t % 2)
            tile_loop(sp, save)
            for t in range(LOOP1, T):
                save(t, t % 2)

            sp.wait_ge(S["scattered"], 16 * 2 * T)
            for t in range(XS_RING):
                sp.dma_start(xs[:, t, :], xs_dram[t * P:(t + 1) * P, :]).then_inc(xs_in[t], 16)

            def load(t, c, i, r, static):
                if not static or t + XS_RING < ET:
                    sp.wait_ge(ys_sent[c % YS_RING], (r + 1) * 16)
                    sp.dma_start(xs[:, c, :], xs_dram[bass.ds((t + XS_RING) * P, P), :]).then_inc(xs_in[c], 16)

            for t in range(XS_RING):
                load(t, t, 0, t // YS_RING, True)
            with sp.Fori(1, ELOOP // XS_RING - 1) as i:
                for c in range(XS_RING):
                    load(i * XS_RING + c, c, i, i * (XS_RING // YS_RING) + c // YS_RING, False)
            for t in range(ELOOP - XS_RING, ET):
                load(t, t % XS_RING, t // XS_RING, t // YS_RING, True)

            for slot in range(YS_RING):
                sp.wait_ge(ys_sent[slot], 16 * len(range(slot, ET, YS_RING)))
            for q in range(T // G4):
                for c, buf in enumerate((first, second)):
                    sp.dma_start(buf[:, q * G4:(q + 1) * G4, :],
                                 results_dram[c * T * P:(c + 1) * T * P, :].rearrange("(p t) d -> p t d", p=P)[
                                     :, q * G4:(q + 1) * G4, :]).then_inc(results_in[q], 16)

            out_rows = rows(out)
            stores = [(q * G4, G4) for q in range(T // G4 - 1)] + [(T - G4, G4 // 2), (T - G4 // 2, G4 // 2)]
            for n, (t, size) in enumerate(stores):
                sp.wait_ge(S["combined"], n + 1)
                b, tb = t // TB, t % TB
                sp.dma_start(out_rows[:, b, tb:tb + size, :], x_all[:, t:t + size, :]).then_inc(S["out_stored"], 16)
            sp.wait_ge(S["out_stored"], 16 * len(stores))

        @block.gpsimd
        def _(pool):
            link = [0]

            def linked(ins):
                link[0] += 1
                ins.then_inc(S["pool_link"], 1)
                pool.wait_ge(S["pool_link"], link[0])

            pool.memset(kt_sb[:, :, :, :, :], 0.0).then_inc(S["blocks_cleared"], 1)
            pool.memset(ident[:, :], 0.0).then_inc(S["ident_cleared"], 1)
            pool.memset(filler[:, :], 0.0).then_inc(S["filler_set"], 1)
            linked(pool.memset(spare[:, :, :], 0.0))
            pool.iota(spare[:, :, 0].bitcast(I32), pattern=[[P, ET]], base=2 * T * P, channel_multiplier=1).then_inc(S["filler_set"], 1)
            pool.wait_ge(S["ident_cleared"], 1)
            pool.affine_select(out=ident[:, :], in_=ident[:, :], compare_op=ALU.not_equal, fill=1.0, base=0,
                               pattern=[[-1, P]], channel_multiplier=1).then_inc(S["ident_set"], 1)
            pool.memset(scratch[:, :], 0.0).then_inc(S["blocks_cleared"], 1)
            linked(pool.memset(head0[:, :], 0.0))
            pool.memset(head0[:, 0:M], 1.0).then_inc(S["head0_set"], 1)
            pool.memset(xn2_all[:, :, D:XW], 0.0).then_inc(S["rows_set"], 1)
            pool.iota(result_row[:, :], pattern=[[1, T]], base=0, channel_multiplier=T).then_inc(S["rows_set"], 1)

            def newton(t, par):
                v, hv, y, w = (z[:, par:par + 1] for z in (var2, half2, rstd2, newton2))
                pool.wait_ge(S["guess2_set"], t + 1)
                for s in range(NEWTON):
                    pool.tensor_tensor(w, y, y, ALU.mult)
                    if s == 0:
                        pool.tensor_scalar(hv, v, -0.5, None, ALU.mult)
                    pool.drain()
                    pool.tensor_scalar(w, w, hv, 1.5, ALU.mult, ALU.add)
                    pool.drain()
                    last = pool.tensor_tensor(y, y, w, ALU.mult)
                    if s < NEWTON - 1:
                        pool.drain()
                last.then_inc(S["rstd2_set"], 1)

            def normalize(t, par):
                pool.wait_ge(S["recip_set"], t + 1)
                p3 = probs[:, par, :].rearrange("p (h m) -> p h m", h=H)
                pool.tensor_tensor(p3, p3, srec[:, par, :].unsqueeze(2).to_broadcast([P, H, M]),
                                   ALU.mult).then_inc(S["probs_set"], 1)

            normalize(0, 0)

            def step(t, par, static=False):
                if not static or t + 1 < T:
                    normalize(t + 1, 1 - par)
                if not static or 1 <= t <= T:
                    newton(t - 1, 1 - par)

            for t in range(LOOP0):
                step(t, t % 2, True)
            tile_loop(pool, step)
            for t in range(LOOP1, T + 1):
                step(t, t % 2, True)

            linked(pool.iota(rank_first[:, :], pattern=[[-1, E]], base=E, channel_multiplier=0,
                             allow_small_or_imprecise_dtypes=True))
            pool.iota(step_rows[:, :], pattern=[[P, T]], base=0, channel_multiplier=0,
                      allow_small_or_imprecise_dtypes=True).then_inc(S["consts_set"], 1)
            pool.iota(tile_no[:, :], pattern=[[1, ET]], base=0, channel_multiplier=0,
                      allow_small_or_imprecise_dtypes=True).then_inc(S["consts_set"], 1)
            linked(pool.memset(before[:, :, :], 1.0))
            linked(pool.memset(earlier[:, :], 1.0))
            pool.memset(ones[:, :], 1.0).then_inc(S["consts_set"], 1)
            pool.affine_select(out=before[:, :, :], in_=before[:, :, :], compare_op=ALU.is_gt, fill=0.0, base=0,
                               pattern=[[1, E], [-1, E]], channel_multiplier=0).then_inc(S["consts_set"], 1)
            pool.affine_select(out=earlier[:, :], in_=earlier[:, :], compare_op=ALU.is_gt, fill=0.0, base=0,
                               pattern=[[1, P]], channel_multiplier=-1).then_inc(S["consts_set"], 1)

            for c in range(2):
                pool.wait_ge(xn2_saved[c], 16 * (T // 2))
            pool.wait_ge(S["rows_filled"], 32)
            pool.wait_ge(S["pos_set"], 1)
            for c in range(2):
                if c == 1:
                    pool.wait_ge(S["scattered"], 16 * T)
                if c == 0:
                    pool.wait_ge(S["rows_set"], 2)
                    pool.wait_ge(S["weights_set"], 1)
                pool.tensor_copy(xn2_all[:, :, D + 1], w12[:, c, :]).then_inc(S["rows_set"], 1)
                pool.tensor_scalar(xn2_all[:, :, D].bitcast(I32), result_row[:, :], float(c * T * P), None,
                                   ALU.add).then_inc(S["rows_set"], 1)
                pool.wait_ge(S["rows_set"], 2 * c + 4)
                for t in range(T):
                    pool.indirect_dma_start(xs_dram, bass.IndirectOffsetOnAxis(pos[:, c, t:t + 1], 0),
                                            xn2_all[:, t, :], None).then_inc(S["scattered"], 16)

            for t in range(ET):
                pool.wait_ge(S["ys_set"], t + 1)
                pool.indirect_dma_start(results_dram, bass.IndirectOffsetOnAxis(xs[:, t % XS_RING, D:D + 1].bitcast(U32), 0),
                                        ys[:, t % YS_RING, :], None).then_inc(ys_sent[t % YS_RING], 16)

            for q in range(T // G4 - 1):
                group = slice(q * G4, (q + 1) * G4)
                pool.wait_ge(results_in[q], 32)
                pool.tensor_tensor(first[:, group, :], first[:, group, :], second[:, group, :],
                                   ALU.add).then_inc(S["choices_added"], 1)

        @block.tensor
        def _(pe):
            mm, transpose = nc.tensor.matmul, nc.tensor.transpose

            def kv_t(w, ps_of, ready):
                for j in range(PAIRS):
                    for k in range(KD):
                        last = mm(ps_of(j), w[:, k, j * P:(j + 1) * P], ctx_sb[:, k, :],
                                  start=(k == 0), stop=(k == KD - 1))
                    last.then_inc(ready, 1)

            def fold_q(n):
                b, k = n // KD, n % KD
                if n > KD:
                    pe.wait_ge(S["g_set_dve"], n)
                    pe.wait_ge(S["g_set_act"], n)
                if n == KD:
                    pe.wait_ge(S["vo_set"], KC)
                for j in range(PAIRS):
                    c = (j % 2) * 2 * M
                    last = mm(g_ps(n)[:, j // 2, c:c + 2 * M], wqt_sb[:, j, k * P:(k + 1) * P],
                              kt_sb[:, j, b, :, :].rearrange("p a m -> p (a m)"), start=True, stop=True)
                last.then_inc(S["g_in_ps"], 1)

            def fold_o(b):
                for c in range(KC):
                    n = b * KC + c
                    if n >= 2:
                        pe.wait_ge(S["vo_set"], n - 1)
                    pairs = [j for j in range(PAIRS) if j * 2 * M < c * P + KEYS[c] and (j + 1) * 2 * M > c * P]
                    for j in pairs:
                        last = mm(vo_ps(n)[0:KEYS[c], :], vt_sb[:, j, b, c * P:c * P + KEYS[c]], wo_sb[:, j, :],
                                  start=(j == pairs[0]), stop=(j == pairs[-1] and c > 0))
                    if c == 0:
                        last = mm(vo_ps(n)[0:KEYS[c], :], head0[:, :], bo_sb[:, :], start=False, stop=True)
                    last.then_inc(S["vo_in_ps"], 1)

            def turn_x(t, par, static=False):
                pe.wait_ge(S["xn1_set"], t + 1)
                if not static or t >= 3:
                    pe.wait_ge(S["pt_set_dve"], t - 2)
                if static and 1 <= t < 3:
                    pe.wait_ge(S["xt_set"], t)
                for k in range(KD):
                    last = transpose(turned[:, 1, (k + 1) * P:(k + 2) * P], xn1[:, par, k * P:(k + 1) * P], ident[:, :])
                last.then_inc(S["xt_in_ps"], 1)

            def scores(t, par, static=False):
                pe.wait_ge(S["xt_set"], t + 1)
                if not static or t >= 2:
                    pe.wait_ge(S["shifted"], t - 1)
                for half in range(2):
                    for k in range(KD):
                        last = mm(quad[:, par, half, 0:HALF], xt[:, par, k, :],
                                  g_sb[:, t // TB, k, half * HALF:(half + 1) * HALF],
                                  start=(k == 0), stop=(k == KD - 1))
                last.then_inc(S["scores_in_ps"], 1)

            def turn_probs(t, par, static=False):
                pe.wait_ge(S["probs_set"], t + 1)
                if not static or t >= 1:
                    pe.wait_ge(S["pt_set_act"], t)
                if not static or t + 2 < T:
                    pe.wait_ge(S["xt_set"], t + 3)
                for c in range(KC):
                    last = transpose(turned_flat[0:KEYS[c], c * P:(c + 1) * P], probs[:, par, c * P:c * P + KEYS[c]], ident[:, :])
                last.then_inc(S["pt_in_ps"], 1)

            def attend(t, par, static=False):
                pe.wait_ge(S["pt_set_act"], t + 1)
                pe.wait_ge(S["pt_set_dve"], t + 1)
                if not static or t >= 1:
                    pe.wait_ge(S["x2_set"], t)
                for c in range(KC):
                    last = mm(result_x, pt_sb[0:KEYS[c], c, :], vo_sb[0:KEYS[c], t // TB, c, :],
                              start=(c == 0), stop=(c == KC - 1))
                last.then_inc(S["attn_in_ps"], 1)

            def turn_xn2(t, par, static=False):
                pe.wait_ge(S["xn2_set"], t + 1)
                if not static or t >= 1:
                    pe.wait_ge(S["xn2t_set"], t)
                for k in range(KD):
                    last = transpose(result[:, 1, k * P:(k + 1) * P], xn2[:, par, k * P:(k + 1) * P], ident[:, :])
                last.then_inc(S["xn2t_in_ps"], 1)

            pe.wait_ge(S["kv_w_in"], 32)
            kv_t(wk_sb, lambda j: quad[:, j // 2, j % 2, 0:B * M], S["kt_in_ps"])
            pe.wait_ge(S["wv_in"], 16)
            kv_t(wv_sb, vt_ps, S["vt_in_ps"])
            pe.wait_ge(S["wq_in"], 16)
            pe.wait_ge(S["kt_set"], 2 * PAIRS)
            fold_q(0)
            pe.wait_ge(S["ident_set"], 1)
            pe.wait_ge(S["vt_set"], 2 * PAIRS)
            turn_x(0, 0, True)
            fold_q(1)
            turn_x(1, 1, True)
            pe.wait_ge(S["g_set_dve"], KD)
            pe.wait_ge(S["g_set_act"], KD)
            scores(0, 0, True)
            pe.wait_ge(S["wo_in"], 16)
            pe.wait_ge(S["bo_in"], 16)
            pe.wait_ge(S["head0_set"], 1)
            fold_o(0)
            fold_q(2)
            turn_x(2, 0, True)
            fold_q(3)
            pe.wait_ge(S["g_set_dve"], B * KD)
            fold_o(1)
            scores(1, 1, True)
            pe.wait_ge(S["g_set_dve"], B * KD)
            pe.wait_ge(S["g_set_act"], B * KD)
            pe.wait_ge(S["vo_set"], B * KC)

            def step(t, par, static=False):
                turn_probs(t, par, static)
                if not static or t + 2 < T:
                    scores(t + 2, par, static)
                if not static or t + 3 < T:
                    turn_x(t + 3, 1 - par, static)
                attend(t, par, static)
                if not static or t >= 2:
                    turn_xn2(t - 2, par, static)

            def logits(g):
                pe.wait_ge(S["xn2t_set"], G4 * (g + 1))
                if g >= 2:
                    pe.wait_ge(S["lt_set"], g - 1)
                for k in range(KD):
                    last = mm(quad[0:NR, 0, g % 2, :], wr_sb[:, k, :], x2t_all[:, k, g * GT:(g + 1) * GT],
                              start=(k == 0), stop=(k == KD - 1))
                last.then_inc(S["lt_in_ps"], 1)

            def turn_logits(g):
                pe.wait_ge(S["lt_set"], g + 1)
                for t in range(G4 * g, G4 * (g + 1)):
                    last = transpose(turned[:, 0, t * SCORE_W:t * SCORE_W + NR], lt_sb[:, t * P:(t + 1) * P], ident[0:NR, 0:NR])
                last.then_inc(S["logits_in_ps"], 1)

            for t in range(LOOP0):
                step(t, t % 2, True)
            tile_loop(pe, step)
            for t in range(LOOP1, T - 1):
                step(t, t % 2, True)
            pe.wait_ge(S["wr_in"], 16)
            pe.wait_ge(S["shifted"], T)
            logits(0)
            step(T - 1, 1, True)
            logits(1)
            turn_xn2(T - 2, 0, True)
            logits(2)
            turn_logits(0)
            turn_logits(1)
            turn_xn2(T - 1, 1, True)
            turn_logits(2)
            logits(3)
            turn_logits(3)

            def shared_in(g, slices=range(SJ)):
                for j in slices:
                    n = g * SJ + j
                    if n >= 2:
                        pe.wait_ge(S["hs_set"], n - 1)
                    for half, ready in ((0, S["gate_in_ps"]), (1, S["up_in_ps"])):
                        for k in range(KD):
                            c = half * SHID + j * P
                            last = mm(quad[:, j % 2, half, :], wsi_sb[:, k, c:c + P], x2t_all[:, k, g * GT:(g + 1) * GT],
                                      start=(k == 0), stop=(k == KD - 1))
                        last.then_inc(ready, 1)

            def shared_out(g):
                pe.wait_ge(S["hs_set"], (g + 1) * SJ)
                for t in range(G4):
                    n = g * G4 + t
                    if n >= 2:
                        pe.wait_ge(S["shared_added"], n - 1)
                    for j in range(SJ):
                        last = mm(result[:, t % 2, 0:D], hs[:, g % 2, j, t * P:(t + 1) * P], wso_sb[:, j, :],
                                  start=(j == 0), stop=(j == SJ - 1))
                    last.then_inc(S["down_in_ps"], 1)

            pe.wait_ge(S["ws_in"], 32)
            shared_in(0, range(2))

            pe.wait_ge(S["consts_set"], 5)
            pe.wait_ge(S["picked_set"], 1)
            ranks = turned[:, 1, 0:T * E]
            mm(ranks, earlier[:, :], picked[:, :, :].rearrange("p t e -> p (t e)"), start=True, stop=False)
            for t in range(T - 1):
                later = T - 1 - t
                last = mm(turned[:, 1, (t + 1) * E:T * E].rearrange("p (t e) -> p t e", e=E), ones[:, :],
                          picked[:, t, :].unsqueeze(1).to_broadcast([P, later, E]), start=False, stop=(t == T - 2))
            last.then_inc(S["ranks_in_ps"], 1)
            pe.wait_ge(S["picked_t_set"], 1)
            mm(result[:, 1, 0:E], ones[:, :], picked_t[:, :], start=True, stop=True).then_inc(S["counts_in_ps"], 1)

            shared_in(0, range(2, SJ))
            shared_in(1)
            shared_out(0)
            shared_in(2)
            shared_out(1)
            shared_out(2)

            experts = we_sb[:, :, :].rearrange("p e n -> p (e n)")

            def weights_at(t):
                return pe.value_load(expert_off[0:1, bass.ds(t, 1)], min_val=0, max_val=(E - 1) * EW)

            def turn_xs(t, slot, par, load_no):
                pe.wait_ge(xs_in[slot], load_no * 16)
                for k in range(KD):
                    last = transpose(turned[:, par, k * P:(k + 1) * P], xs[:, slot, k * P:(k + 1) * P], ident[:, :])
                last.then_inc(S["xst_in_ps"], 1)

            def expert_in(t, par, off):
                pe.wait_ge(S["xst_set"], t + 1)
                for k in range(KD):
                    last = mm(quad[:, 0, par, 0:2 * P], xst[:, par, k, :], experts[:, bass.ds(off + k * 2 * P, 2 * P)],
                              start=(k == 0), stop=(k == KD - 1))
                last.then_inc(S["gu_in_ps"], 1)

            def turn_h(t, par):
                pe.wait_ge(S["eh_set"], t + 1)
                transpose(quad[:, 1, par, 0:P], eh[:, par, :], ident[:, :]).then_inc(S["eht_in_ps"], 1)

            def expert_out(t, par, off, static=False):
                pe.wait_ge(S["eht_set"], t + 1)
                if not static or t >= 2:
                    pe.wait_ge(S["ys_set"], t - 1)
                mm(result[:, par, 0:D], eht[:, par, :], experts[:, bass.ds(off + KD * 2 * P, D)],
                   start=True, stop=True).then_inc(S["y_in_ps"], 1)

            pe.wait_ge(S["experts_set"], 1)
            pe.wait_ge(S["we_in"], 16)
            off0, off1 = weights_at(0), weights_at(1)
            turn_xs(0, 0, 0, 1)
            turn_xs(1, 1, 1, 1)
            expert_in(0, 0, off0)
            turn_xs(2, 2, 0, 1)
            expert_in(1, 1, off1)
            pe.wait_ge(S["shared_added"], 3 * G4)

            offs = {}

            def expert_step(t, c, i, r, static):
                more = not static or t + 2 < ET
                if c == 0:
                    offs.clear()
                    offs[2] = weights_at(t + 2)
                turn_h(t, c % 2)
                if not static or t + 3 < ET:
                    turn_xs(t + 3, (c + 3) % XS_RING, (c + 1) % 2, i + ((c + 3) // XS_RING + 1))
                if more:
                    expert_in(t + 2, c % 2, offs[c + 2])
                if c < 2:
                    offs[c] = weights_at(t)
                if c + 1 < XS_RING and (not static or t + 3 < ET):
                    offs[c + 3] = weights_at(t + 3)
                expert_out(t, c % 2, offs[c], static)

            expert_steps(pe, expert_step)

            pe.wait_ge(S["ys_set"], ET)
            shared_in(3)
            shared_out(3)

        @block.scalar
        def _(act):
            copy = nc.scalar.copy
            act.dma_start(x_all[:, 0:G4, :], rows(x)[:, 0, 0:G4, :]).then_inc(x_in[0], 16)
            act.dma_start(bo_sb[:, :], bo.unsqueeze(0)).then_inc(S["bo_in"], 16)

            act.wait_ge(S["blocks_cleared"], 2)
            for j in range(PAIRS):
                act.wait_ge(S["vt_in_ps"], j + 1)
                for a in range(2):
                    q = slice(a * P // 2, (a + 1) * P // 2)
                    at = (2 * j + a) * M
                    copy(vt_sb[q, j, :, at:at + M],
                         vt_ps(j)[q, :].rearrange("p (b m) -> p b m", b=B)).then_inc(S["vt_set"], 1)

            def g_out(n):
                act.wait_ge(S["g_in_ps"], n + 1)
                copy(g_sb[:, n // KD, n % KD, HALF:HM], g_ps(n)[:, 1, 0:HALF]).then_inc(S["g_set_act"], 1)

            def xt_out(t, par, static=False):
                act.wait_ge(S["xt_in_ps"], t + 1)
                if not static or t >= 2:
                    act.wait_ge(S["scores_in_ps"], t - 1)
                copy(xt[:, par, :, :].rearrange("p k c -> p (k c)"), turned[:, 1, P:P + D]).then_inc(S["xt_set"], 1)

            def vo_out(n):
                act.wait_ge(S["vo_in_ps"], n + 1)
                b, c = n // KC, n % KC
                copy(vo_sb[0:KEYS[c], b, c, :], vo_ps(n)[0:KEYS[c], :]).then_inc(S["vo_set"], 1)

            def exps(t, par, static=False):
                act.wait_ge(S["shifted"], t + 1)
                nc.scalar.activation(probs[:, par, :], probs[:, par, :], ACT.Exp, scale=SCALE).then_inc(S["exps_set"], 1)

            g_out(0)
            xt_out(0, 0, True)
            g_out(1)
            xt_out(1, 1, True)
            for c in range(KC):
                vo_out(c)
            g_out(2)
            xt_out(2, 0, True)
            g_out(3)
            exps(0, 0)
            for c in range(KC):
                vo_out(KC + c)

            def pt_out(t):
                act.wait_ge(S["pt_in_ps"], t + 1)
                copy(pt_sb[:, 0:KC - 1, :].rearrange("p c k -> p (c k)"), turned[:, 0, :]).then_inc(S["pt_set_act"], 1)

            def xn2t_out(t):
                act.wait_ge(S["xn2t_in_ps"], t + 1)
                copy(x2t_all[:, :, bass.ds(t * P, P)],
                     result[:, 1, 0:KD * P].rearrange("p (k c) -> p k c", k=KD)).then_inc(S["xn2t_set"], 1)

            def step(t, par, static=False):
                pt_out(t)
                if not static or t + 1 < T:
                    exps(t + 1, 1 - par)
                if not static or t + 3 < T:
                    xt_out(t + 3, 1 - par, static)
                if not static or t >= 2:
                    xn2t_out(t - 2)

            def logits_out(g):
                act.wait_ge(S["lt_in_ps"], g + 1)
                copy(lt_sb[:, g * GT:(g + 1) * GT], quad[0:NR, 0, g % 2, :]).then_inc(S["lt_set"], 1)

            for t in range(LOOP0):
                step(t, t % 2, True)
            tile_loop(act, step)
            for t in range(LOOP1, T):
                step(t, t % 2, True)
            logits_out(0)
            logits_out(1)
            xn2t_out(T - 2)
            logits_out(2)
            xn2t_out(T - 1)
            logits_out(3)

            def shared_tanh(n):
                act.wait_ge(S["gate_in_ps"], n + 1)
                if n >= 2:
                    act.wait_ge(S["ga_set"], n - 1)
                nc.scalar.activation(th[:, n % 2, :], quad[:, n % 2, 0, :], ACT.Tanh, scale=0.5).then_inc(S["tanh_set"], 1)

            act.wait_ge(S["rows_filled"], 32)
            shared_tanh(0)
            act.wait_ge(S["gaps_set"], 1)
            nc.scalar.activation(tgate[:, :], lg[:, :, E], ACT.Tanh, scale=0.5).then_inc(S["tgate_set"], 1)
            nc.scalar.activation(egap[:, :], gap[:, :], ACT.Exp).then_inc(S["egap_set"], 1)
            for n in range(1, 3 * SJ):
                shared_tanh(n)

            def xst_out(t, par, static=False):
                act.wait_ge(S["xst_in_ps"], t + 1)
                if not static or t >= 2:
                    act.wait_ge(S["gu_in_ps"], t - 1)
                copy(xst[:, par, :, :].rearrange("p k c -> p (k c)"), turned[:, par, 0:D]).then_inc(S["xst_set"], 1)

            def expert_tanh(t, par, static=False):
                act.wait_ge(S["gu_in_ps"], t + 1)
                if not static or t >= 2:
                    act.wait_ge(S["ega_set"], t - 1)
                nc.scalar.activation(eth[:, par, :], quad[:, 0, par, 0:P], ACT.Tanh,
                                     scale=0.5).then_inc(S["eth_set"], 1)

            def y_out(t, c, r, static):
                act.wait_ge(S["y_in_ps"], t + 1)
                if not static or t >= YS_RING:
                    act.wait_ge(ys_sent[c % YS_RING], r * 16)
                nc.scalar.activation(ys[:, c % YS_RING, :], result[:, c % 2, 0:D], ACT.Copy,
                                     scale=xs[:, c, D + 1:D + 2]).then_inc(S["ys_set"], 1)

            xst_out(0, 0, True)
            xst_out(1, 1, True)
            expert_tanh(0, 0, True)
            xst_out(2, 0, True)
            expert_tanh(1, 1, True)

            def expert_step(t, c, i, r, static):
                if not static or t + 3 < ET:
                    xst_out(t + 3, (c + 1) % 2)
                if not static or t + 2 < ET:
                    expert_tanh(t + 2, c % 2)
                y_out(t, c, r, static)

            expert_steps(act, expert_step)

            for n in range(3 * SJ, 4 * SJ):
                shared_tanh(n)

        @block.vector
        def _(dve):
            v = nc.vector
            link = [0]

            def linked(ins):
                link[0] += 1
                ins.then_inc(S["dve_link"], 1)
                dve.wait_ge(S["dve_link"], link[0])

            dve.wait_ge(S["blocks_cleared"], 1)
            for j in range(PAIRS):
                dve.wait_ge(S["kt_in_ps"], j + 1)
                for a in range(2):
                    q = slice(a * P // 2, (a + 1) * P // 2)
                    v.tensor_copy(kt_sb[q, j, :, a, :],
                                  quad[q, j // 2, j % 2, 0:B * M].rearrange("p (b m) -> p b m", b=B)).then_inc(S["kt_set"], 1)

            def norm1(t0, t1):
                for t in range(t0, t1):
                    if t % G4 == 0:
                        dve.wait_ge(x_in[t // G4], 16)
                    ins = v.bn_stats(stats[:, t, :], x_all[:, t, :])
                linked(ins)
                for t in range(t0, t1):
                    ins = v.bn_aggr(moments1[:, t, :], stats[:, t, :])
                linked(ins)
                va, y, w = (z[:, t0:t1] for z in (var1, rstd1, newton1))
                linked(v.tensor_scalar(va, moments1[:, t0:t1, 1], LN_EPS, None, ALU.add))
                linked(v.tensor_scalar(w.bitcast(I32), va.bitcast(I32), 1, None, ALU.logical_shift_right))
                linked(v.tensor_scalar(y.bitcast(I32), w.bitcast(I32), -1.0, float(RSQRT_MAGIC), ALU.mult, ALU.add))
                for _ in range(NEWTON):
                    linked(v.tensor_tensor(w, y, y, ALU.mult))
                    linked(v.scalar_tensor_tensor(w, w, -0.5, va, ALU.mult, ALU.mult))
                    linked(v.scalar_tensor_tensor(y, w, 1.5, y, ALU.add, ALU.mult))

            def apply1(t, par, static=False):
                if not static or t >= 2:
                    dve.wait_ge(S["xt_in_ps"], t - 1)
                tt = bass.ds(t, 1)
                v.tensor_scalar(xn1[:, par, :], x_all[:, t, :], moments1[:, t, 0:1], rstd1[:, tt],
                                ALU.subtract, ALU.mult).then_inc(S["xn1_set"], 1)

            def g_out(n):
                dve.wait_ge(S["g_in_ps"], n + 1)
                v.tensor_copy(g_sb[:, n // KD, n % KD, 0:HALF], g_ps(n)[:, 0, 0:HALF]).then_inc(S["g_set_dve"], 1)

            def shift(t, par, static=False):
                s4 = quad[:, par, :, 0:HALF].rearrange("p a (h m) -> p a h m", h=HH)
                mx = smax[:, par, :].rearrange("p (a h) -> p a h", a=2)
                dve.wait_ge(S["scores_in_ps"], t + 1)
                v.tensor_reduce(mx, s4, AX, ALU.max).then_inc(S["max_found"], 1)
                dve.wait_ge(S["max_found"], t + 1)
                if not static or t >= 2:
                    dve.wait_ge(S["pt_in_ps"], t - 1)
                v.tensor_tensor(probs[:, par, :].rearrange("p (a h m) -> p a h m", a=2, h=HH), s4,
                                mx.unsqueeze(3).to_broadcast([P, 2, HH, M]), ALU.subtract).then_inc(S["shifted"], 1)

            def sums(t, par, static=False):
                dve.wait_ge(S["exps_set"], t + 1)
                v.tensor_reduce(ssum[:, par, :], probs[:, par, :].rearrange("p (h m) -> p h m", h=H), AX,
                                ALU.add).then_inc(S["summed"], 1)
                dve.wait_ge(S["summed"], t + 1)
                v.reciprocal(srec[:, par, :], ssum[:, par, :]).then_inc(S["recip_set"], 1)

            norm1(0, G4)
            apply1(0, 0, True)
            apply1(1, 1, True)
            g_out(0)
            g_out(1)
            apply1(2, 0, True)
            shift(0, 0, True)
            g_out(2)
            sums(0, 0, True)
            g_out(3)
            norm1(G4, T)

            def pt_out(t):
                dve.wait_ge(S["pt_in_ps"], t + 1)
                v.tensor_copy(pt_sb[0:KEYS[-1], KC - 1, :], turned[0:KEYS[-1], 1, 0:P]).then_inc(S["pt_set_dve"], 1)

            def residual(t):
                dve.wait_ge(S["attn_in_ps"], t + 1)
                v.tensor_tensor(x_all[:, t, :], result_x, x_all[:, t, :], ALU.add).then_inc(S["x2_set"], 1)

            def norm2(t, par):
                apart(dve)
                dve.wait_ge(S["x2_set"], t + 1)
                v.bn_stats(stats2[:, :], x_all[:, t, :]).then_inc(S["stats2_set"], 1)
                apart(dve)
                dve.wait_ge(S["stats2_set"], t + 1)
                v.bn_aggr(moments2[:, par, :], stats2[:, :]).then_inc(S["moments2_set"], 1)
                va, y, w = (z[:, par:par + 1] for z in (var2, rstd2, newton2))
                dve.wait_ge(S["moments2_set"], t + 1)
                v.tensor_scalar(va, moments2[:, par, 1:2], LN_EPS, None, ALU.add).then_inc(S["var2_set"], 1)
                dve.wait_ge(S["var2_set"], 2 * t + 1)
                v.tensor_scalar(w.bitcast(I32), va.bitcast(I32), 1, None, ALU.logical_shift_right).then_inc(S["var2_set"], 1)
                dve.wait_ge(S["var2_set"], 2 * t + 2)
                v.tensor_scalar(y.bitcast(I32), w.bitcast(I32), -1.0, float(RSQRT_MAGIC), ALU.mult,
                                ALU.add).then_inc(S["guess2_set"], 1)

            def apply2(t, par, static=False):
                dve.wait_ge(S["rstd2_set"], t + 1)
                if not static or t >= 2:
                    dve.wait_ge(S["xn2t_in_ps"], t - 1)
                    dve.wait_ge(xn2_saved[par], 8 * (t - par))
                v.tensor_scalar(xn2[:, par, :], x_all[:, t, :], moments2[:, par, 0:1], rstd2[:, par:par + 1],
                                ALU.subtract, ALU.mult).then_inc(S["xn2_set"], 1)

            def step(t, par, static=False):
                if not static or t + 1 < T:
                    shift(t + 1, 1 - par, static)
                if not static or t < T:
                    pt_out(t)
                if not static or t + 3 < T:
                    apply1(t + 3, 1 - par, static)
                if not static or 1 <= t <= T:
                    residual(t - 1)
                if not static or t + 1 < T:
                    sums(t + 1, 1 - par, static)
                if not static or 1 <= t <= T:
                    norm2(t - 1, 1 - par)
                if not static or t >= 2:
                    apply2(t - 2, par, static)

            for t in range(LOOP0):
                step(t, t % 2, True)
            tile_loop(dve, step)
            for t in range(LOOP1, T + 2):
                step(t, t % 2, True)

            def te(z):
                return z.unsqueeze(2).to_broadcast([P, T, E])

            first_rank = rank_first[:, :].unsqueeze(1).to_broadcast([P, T, E])
            dve.wait_ge(S["logits_in_ps"], T // G4)
            linked(v.tensor_copy(lg[:, :, :], turned[:, 0, 0:T * SCORE_W].rearrange("p (t n) -> p t n", n=SCORE_W)[:, :, 0:NR]))
            dve.wait_ge(S["consts_set"], 5)

            def choose(l, top, oh):
                linked(v.tensor_reduce(top, l, AX, ALU.max))
                linked(v.tensor_tensor(eq[:, :, :], l, te(top), ALU.is_equal))
                linked(v.tensor_tensor(eq[:, :, :], eq[:, :, :], first_rank, ALU.mult))
                linked(v.tensor_reduce(pick[:, :], eq[:, :, :], AX, ALU.max))
                linked(v.tensor_tensor(oh, eq[:, :, :], te(pick[:, :]), ALU.is_equal))

            choose(lg[:, :, 0:E], top1[:, :], oh1[:, :, :])
            linked(v.scalar_tensor_tensor(lg2[:, :, :], oh1[:, :, :], MASKED, lg[:, :, 0:E], ALU.mult, ALU.add))
            choose(lg2[:, :, :], top2[:, :], oh2[:, :, :])
            v.tensor_tensor(gap[:, :], top2[:, :], top1[:, :], ALU.subtract).then_inc(S["gaps_set"], 1)
            v.tensor_tensor(picked[:, :, :], oh1[:, :, :], oh2[:, :, :], ALU.add).then_inc(S["picked_set"], 1)
            dve.wait_ge(S["picked_set"], 1)
            with nc.allow_low_precision(reason="counts up to 16 are exact in bfloat16"):
                v.tensor_reduce(picked_t[:, :], picked[:, :, :].rearrange("p t e -> p e t"), AX, ALU.add).then_inc(S["picked_t_set"], 1)

            def shared_h(n):
                g, j = n // SJ, n % SJ
                dve.wait_ge(S["tanh_set"], n + 1)
                v.scalar_tensor_tensor(ga[:, n % 2, :], th[:, n % 2, :], 1.0, quad[:, j % 2, 0, :], ALU.add,
                                       ALU.mult).then_inc(S["ga_set"], 1)
                dve.wait_ge(S["ga_set"], n + 1)
                dve.wait_ge(S["up_in_ps"], n + 1)
                if g >= 2:
                    dve.wait_ge(S["down_in_ps"], (g - 1) * G4)
                v.tensor_tensor(hs[:, g % 2, j, :], ga[:, n % 2, :], quad[:, j % 2, 1, :], ALU.mult).then_inc(S["hs_set"], 1)

            for n in range(2):
                shared_h(n)

            dve.wait_ge(S["egap_set"], 1)
            linked(v.tensor_scalar(gap[:, :], egap[:, :], 2.0, 2.0, ALU.mult, ALU.add))
            linked(v.reciprocal(w12[:, 0, :], gap[:, :]))
            v.tensor_tensor(w12[:, 1, :], w12[:, 0, :], egap[:, :], ALU.mult).then_inc(S["weights_set"], 1)

            dve.wait_ge(S["counts_in_ps"], 1)
            linked(v.tensor_copy(counts[:, :], result[:, 1, 0:E]))
            linked(v.tensor_tensor(eq[:, 0:E, :], counts[:, :].unsqueeze(2).to_broadcast([P, E, T]),
                                   step_rows[:, :].unsqueeze(1).to_broadcast([P, E, T]), ALU.is_gt))
            linked(v.tensor_reduce(ntiles[:, :], eq[:, 0:E, :], AX, ALU.add))
            linked(v.tensor_tensor(lg2[:, 0:E, :], before[:, :, :], ntiles[:, :].unsqueeze(1).to_broadcast([P, E, E]), ALU.mult))
            linked(v.tensor_reduce(base[:, :], lg2[:, 0:E, :], AX, ALU.add))
            linked(v.tensor_scalar(base_row[:, :], base[:, :], float(P), None, ALU.mult))
            linked(v.tensor_tensor(lg2[:, :, :], turned[:, 1, 0:T * E].rearrange("p (t e) -> p t e", e=E),
                                   base_row[:, :].unsqueeze(1).to_broadcast([P, T, E]), ALU.add))
            for c, oh in enumerate((oh1, oh2)):
                linked(v.tensor_tensor(eq[:, :, :], oh[:, :, :], lg2[:, :, :], ALU.mult))
                linked(v.tensor_reduce(posf[:, c, :], eq[:, :, :], AX, ALU.add))
            v.tensor_copy(pos[:, :, :], posf[:, :, :]).then_inc(S["pos_set"], 1)
            linked(v.tensor_tensor(base_end[:, :], base[:, :], ntiles[:, :], ALU.add))
            linked(v.tensor_tensor(past[:, :, :], base_end[0:1, :].unsqueeze(1).to_broadcast([1, ET, E]),
                                   tile_no[:, :].unsqueeze(2).to_broadcast([1, ET, E]), ALU.is_le))
            linked(v.tensor_reduce(ewf[:, :], past[:, :, :], AX, ALU.add))
            linked(v.tensor_scalar(ewf[:, :], ewf[:, :], float(E - 1), float(EW), ALU.min, ALU.mult))
            v.tensor_copy(expert_off[:, :], ewf[:, :]).then_inc(S["experts_set"], 1)
            dve.wait_ge(S["tgate_set"], 1)
            linked(v.tensor_scalar(sgate[:, :], tgate[:, :], 0.25, 0.25, ALU.mult, ALU.add))

            def add_shared(t):
                dve.wait_ge(S["down_in_ps"], t + 1)
                v.scalar_tensor_tensor(x_all[:, t, :], result[:, t % 2, 0:D], sgate[:, t:t + 1],
                                       x_all[:, t, :], ALU.mult, ALU.add).then_inc(S["shared_added"], 1)

            for n in range(2, 2 * SJ):
                shared_h(n)
            for t in range(G4):
                add_shared(t)
            for n in range(2 * SJ, 3 * SJ):
                shared_h(n)
            for t in range(G4, 3 * G4):
                add_shared(t)

            def expert_h(t, par, static=False):
                dve.wait_ge(S["eth_set"], t + 1)
                v.scalar_tensor_tensor(ega[:, par, :], eth[:, par, :], 1.0, quad[:, 0, par, 0:P], ALU.add,
                                       ALU.mult).then_inc(S["ega_set"], 1)
                dve.wait_ge(S["ega_set"], t + 1)
                if not static or t >= 2:
                    dve.wait_ge(S["eht_in_ps"], t - 1)
                v.tensor_tensor(eh[:, par, :], ega[:, par, :], quad[:, 0, par, P:2 * P], ALU.mult).then_inc(S["eh_set"], 1)

            def eht_out(t, par, static=False):
                dve.wait_ge(S["eht_in_ps"], t + 1)
                if not static or t >= 2:
                    dve.wait_ge(S["y_in_ps"], t - 1)
                v.tensor_copy(eht[:, par, :], quad[:, 1, par, 0:P]).then_inc(S["eht_set"], 1)

            expert_h(0, 0, True)
            expert_h(1, 1, True)

            def expert_step(t, c, i, r, static):
                eht_out(t, c % 2, static)
                if not static or t + 2 < ET:
                    expert_h(t + 2, c % 2)

            expert_steps(dve, expert_step)

            def combine(t, size, results):
                v.tensor_tensor(x_all[:, t:t + size, :], x_all[:, t:t + size, :], results[:, t:t + size, :],
                                ALU.add).then_inc(S["combined"], 1)

            def combine_group(q):
                dve.wait_ge(S["choices_added"], q + 1)
                dve.wait_ge(S["shared_added"], (q + 1) * G4)
                combine(q * G4, G4, first)

            last = T - G4
            shared_h(3 * SJ)
            shared_h(3 * SJ + 1)
            shared_h(3 * SJ + 2)
            combine_group(0)
            shared_h(3 * SJ + 3)
            combine_group(1)
            add_shared(last)
            add_shared(last + 1)
            combine_group(2)
            add_shared(last + 2)
            add_shared(last + 3)
            dve.wait_ge(results_in[T // G4 - 1], 32)
            dve.wait_ge(S["shared_added"], T)
            v.tensor_tensor(x_all[:, last:T, :], x_all[:, last:T, :], first[:, last:T, :], ALU.add).then_inc(S["first_added"], 1)
            dve.wait_ge(S["first_added"], 1)
            combine(last, G4 // 2, second)
            combine(T - G4 // 2, G4 // 2, second)


def kernel(**inputs):
    import numpy as np
    import concourse.bacc as bacc
    from concourse.bass_utils import run_bass_kernel_spmd

    a = {k: np.asarray(v) for k, v in inputs.items()}
    x, c = a["x"], a["ctx_1024"]
    B, N, D = x.shape
    M = c.shape[1]
    gate, up, down = a["L0_ffn_We_gate"], a["L0_ffn_We_up"], a["L0_ffn_We_down"]
    E, HID, _ = gate.shape
    KD = D // P
    gu = np.concatenate([gate, up], axis=1).transpose(0, 2, 1).reshape(E, KD, P, 2 * HID)
    w_expert = np.concatenate([gu[:, k] for k in range(KD)] + [down.transpose(0, 2, 1)], axis=2)
    arrays = {
        "x": x,
        "ctx_t": c.transpose(2, 0, 1).reshape(D, B * M),
        "wk": a["L0_xattn_Wk"],
        "wv": a["L0_xattn_Wv"],
        "wq_t": a["L0_xattn_Wq"].T,
        "wo": a["L0_xattn_Wo"],
        "bo": a["L0_xattn_bo"],
        "w_router": np.concatenate([a["L0_ffn_Wg"], a["L0_ffn_Wsg"]], axis=0).T,
        "w_expert": w_expert,
        "w_shared_in": np.concatenate([a["L0_ffn_Ws_gate"], a["L0_ffn_Ws_up"]], axis=0).T,
        "w_shared_out": a["L0_ffn_Ws_down"].T,
    }
    nc = bacc.Bacc("TRN2", target_bir_lowering=False, num_devices=1)
    named, args = {}, []
    for name, v in arrays.items():
        v = np.ascontiguousarray(v)
        named[f"in_{name}"] = v
        args.append(nc.dram_tensor(f"in_{name}", v.shape, mybir.dt.from_np(v.dtype), kind="ExternalInput").ap())
    args.append(nc.dram_tensor("out_x", (B, N, D), F32, kind="ExternalOutput").ap())
    build(nc, *args)
    r = run_bass_kernel_spmd(nc, [named], core_ids=[0])
    return r.results[0]["out_x"]
```

```python
from contextlib import ExitStack

import concourse.bass as bass
from concourse import mybir

ALU = mybir.AluOpType
ACT = mybir.ActivationFunctionType
AX = mybir.AxisListType.X
F32 = mybir.dt.float32
F32R = mybir.dt.float32r
BF16 = mybir.dt.bfloat16
I32 = mybir.dt.int32
U32 = mybir.dt.uint32

P = 128
BANK = 512
XS_RING = 8
YS_RING = 4
LN_EPS = 1e-5
RSQRT_MAGIC = 0x5F3759DF
NEWTON = 3
MASKED = -3.0e38


HIGH, LOW = 0, 1
PASSES = ((HIGH, HIGH), (HIGH, LOW), (LOW, HIGH))


def build(nc, x, ctx_t, wk, wv, wq_t, wo, bo, w_router, w_expert, w_shared_in, w_shared_out, out):
    B, N, D = x.shape
    KD = D // P
    INNER = wk.shape[1]
    PAIRS = INNER // P
    M = ctx_t.shape[1] // B
    H = 2 * PAIRS
    HM = H * M
    HALF = HM // 2
    HH = H // 2
    KEYS = [min(P, HM - c) for c in range(0, HM, P)]
    KC = len(KEYS)
    SCALE = float(INNER // H) ** -0.5
    TB = N // P
    T = B * TB
    E = w_expert.shape[0]
    EW = w_expert.shape[2]
    NR = w_router.shape[1]
    SJ = w_shared_out.shape[0] // P
    SHID = SJ * P
    G4 = 4
    GT = G4 * P
    SG = 2
    ST = SG * P
    NG = T // SG
    NG_FIRST = NG - 1
    ADDED = T // G4 - 1
    ET = 2 * T + E - 1
    SCORE_W = NR + 1

    XW = D + 4
    xs_dram = nc.dram_tensor("tokens_by_expert", (ET * P, XW), F32, kind="Internal").ap()
    results_dram = nc.dram_tensor("results", ((2 * T + ET) * P, D), F32, kind="Internal").ap()

    LOOP0, LOOP1 = 4, T - 4

    with ExitStack() as ctx:
        def sb(name, shape, dt=F32):
            return ctx.enter_context(nc.sbuf_tensor(name, shape, dt))

        def psum(name, shape):
            return ctx.enter_context(nc.psum_tensor(name, shape, F32))

        def sem(name):
            return ctx.enter_context(nc.semaphore(name))

        x_all = sb("x_all", [P, T, D])
        xn2_all = sb("xn2_all", [P, T, XW])
        x2t_high = sb("x2t_high", [P, KD, T * P], F32R)
        with ExitStack() as early:
            def early_sb(name, shape, dt=F32):
                return early.enter_context(nc.sbuf_tensor(name, shape, dt))

            vt_all = early_sb("vt_all", [P, PAIRS * B * KC * P])
            attn_w = early_sb("attn_w", [P, 4, KD * INNER])
            kt_sb = early_sb("kt_sb", [P, PAIRS, B, 2, M])
            ctx_sb = early_sb("ctx_sb", [P, KD, B * M])
            bo_sb = early_sb("bo_sb", [1, D])
            head0 = early_sb("head0", [1, P])
            early_sb("unused", [P, KD * 2 * SHID - PAIRS * B * 2 * M - (KD * B * M + 7) // 8 * 8 - D - P])
            g_high = early_sb("g_high", [P, B, KD, HM], F32R)
            vo_sb = early_sb("vo_sb", [P, B, KC, D])
            ws_raw = early_sb("ws_raw", [P, KD * 2 * SHID + SJ * D])
            g_low = early_sb("g_low", [P, B, KD, HM], F32R)
            filler = early_sb("filler", [P, D])
        low = sb("low", [P, KD * T * P + SJ * D], F32R)
        hs = sb("hs", [P, 2, 2, SJ, ST], F32R)
        wsi_low = sb("wsi_low", [P, KD, 2 * SHID], F32R)
        expert_bufs = sb("expert_bufs", [P, B * KD * HM + B * KC * D])
        we_sb = sb("we_sb", [P, E, EW])
        wr_sb = sb("wr_sb", [P, KD, NR])
        wr_high = sb("wr_high", [P, KD, NR], F32R)
        wr_low = sb("wr_low", [P, KD, NR], F32R)
        wsi_high = sb("wsi_high", [P, KD, 2 * SHID], F32R)
        wso_high = sb("wso_high", [P, SJ, D], F32R)
        ident = sb("ident", [P, P])
        stats = sb("stats", [P, T, 6])
        moments1 = sb("moments1", [P, T, 2])
        var1 = sb("var1", [P, T])
        rstd1 = sb("rstd1", [P, T])
        newton1 = sb("newton1", [P, T])
        stats2 = sb("stats2", [P, 6])
        moments2 = sb("moments2", [P, 2, 2])
        var2 = sb("var2", [P, 2])
        half2 = sb("half2", [P, 2])
        rstd2 = sb("rstd2", [P, 2])
        newton2 = sb("newton2", [P, 2])
        xn1 = sb("xn1", [P, 2, D])
        xt_high = sb("xt_high", [P, 2, KD, P], F32R)
        xt_low = sb("xt_low", [P, 2, KD, P], F32R)
        xn2 = sb("xn2", [P, 2, D])
        smax = sb("smax", [P, 2, H])
        ssum = sb("ssum", [P, 2, H])
        srec = sb("srec", [P, 2, H])
        probs = sb("probs", [P, 2, HM])
        pt_sb = sb("pt_sb", [P, KC, P])
        th = sb("th", [P, 2, ST])
        ga = sb("ga", [P, 2, ST])
        hp = sb("hp", [P, 2, ST])
        lg = sb("lg", [P, T, NR])
        lg2 = sb("lg2", [P, T, E])
        eq = sb("eq", [P, T, E])
        oh1 = sb("oh1", [P, T, E])
        oh2 = sb("oh2", [P, T, E])
        top1 = sb("top1", [P, T])
        top2 = sb("top2", [P, T])
        pick = sb("pick", [P, T])
        picked = sb("picked", [P, T, E], BF16)
        picked_t = sb("picked_t", [P, E], BF16)
        earlier = sb("earlier", [P, P], BF16)
        ones = sb("ones", [P, P], BF16)
        rank_first = sb("rank_first", [P, E])
        result_row = sb("result_row", [P, T], I32)
        step_rows = sb("step_rows", [P, T])
        before = sb("before", [P, E, E])
        tile_no = sb("tile_no", [1, ET])
        counts = sb("counts", [P, E])
        ntiles = sb("ntiles", [P, E])
        base = sb("base", [P, E])
        base_end = sb("base_end", [P, E])
        base_row = sb("base_row", [P, E])
        past = sb("past", [1, ET, E])
        ewf = sb("ewf", [1, ET])
        expert_off = sb("expert_off", [1, ET], I32)
        posf = sb("posf", [P, 2, T])
        pos = sb("pos", [P, 2, T], U32)
        w12 = sb("w12", [P, 2, T])
        gap = sb("gap", [P, T])
        egap = sb("egap", [P, T])
        tgate = sb("tgate", [P, T])
        sgate = sb("sgate", [P, T])

        quad = psum("quad", [P, 2, 2, BANK])
        turned = psum("turned", [P, 2, BANK])
        result = psum("result", [P, 2, BANK])
        turned_flat = turned[:, :, :].rearrange("p a n -> p (a n)")
        result_x = result[:, 0, 0:D]

        vt_sb = vt_all[:, :].rearrange("p (j b c) -> p j b c", j=PAIRS, b=B)
        we_flat = we_sb[:, :, :].rearrange("p e n -> p (e n)")
        second = we_flat[:, 0:T * D].rearrange("p (t d) -> p t d", t=T)
        x2t_low = low[:, 0:KD * T * P].rearrange("p (k c) -> p k c", k=KD)
        wso_low = low[:, KD * T * P:].rearrange("p (j d) -> p j d", j=SJ)
        x2t, wr, wsi, wso = (x2t_high, x2t_low), (wr_high, wr_low), (wsi_high, wsi_low), (wso_high, wso_low)
        gk, xt = (g_high, g_low), (xt_high, xt_low)
        NI = KD * 2 * SHID
        SPLIT = 512
        ws_slices = []
        for c in range(0, NI + SJ * D, SPLIT):
            parts = [w.rearrange("p a b -> p (a b)") for w in
                     ((wsi_high[:, :, :], wsi_low[:, :, :]) if c < NI else (wso_high[:, :, :], wso_low))]
            at = c if c < NI else c - NI
            ws_slices.append((ws_raw[:, c:c + SPLIT], parts[HIGH][:, at:at + SPLIT], parts[LOW][:, at:at + SPLIT]))
        ws_slices.append(tuple(w[:, :, :].rearrange("p k n -> p (k n)") for w in (wr_sb, wr_high, wr_low)))
        SPLITS = [range(n * len(ws_slices) // LOOP0, (n + 1) * len(ws_slices) // LOOP0) for n in range(LOOP0)]
        at = [0]

        def part(n, size):
            view = expert_bufs[:, at[0]:at[0] + n * size].rearrange("p (n c) -> p n c", n=n)
            at[0] += n * size
            return view

        xs, ys = part(XS_RING, XW), part(YS_RING, D)
        xst = part(2, KD * P).rearrange("p n (k c) -> p n k c", k=KD)
        eth, ega, eh, eht = part(2, P), part(2, P), part(2, P), part(2, P)
        first = xn2_all[:, :, 0:D]
        spare = th[:, 0, 0:ET * (XW - D)].rearrange("p (t c) -> p t c", t=ET)
        lt_sb = expert_bufs[0:NR, 0:T * P]
        wk_sb = attn_w[:, 0, :].rearrange("p (k n) -> p k n", k=KD)
        wv_sb = attn_w[:, 1, :].rearrange("p (k n) -> p k n", k=KD)
        wqt_sb = attn_w[:, 2, :].rearrange("p (j n) -> p j n", j=PAIRS)
        wo_sb = attn_w[:, 3, :].rearrange("p (j n) -> p j n", j=PAIRS)

        names = """kv_w_in wv_in wq_in wo_in bo_in wr_in ws_in we_in rows_filled filler_set blocks_cleared
            ident_cleared ident_set kt_in_ps kt_set vt_in_ps vt_set g_in_ps g_high_set g_set vo_in_ps vo_set
            dve_link pool_link consts_set
            xn1_set xt_in_ps xt_high_set xt_set scores_in_ps max_found shifted exps_set summed recip_set probs_set
            pt_in_ps pt_set attn_in_ps x2_set stats2_set moments2_set var2_set halved2_set guess2_set
            rstd2_set xn2_set xn2t_in_ps xn2t_set
            lt_in_ps lt_set logits_in_ps picked_set picked_t_set ranks_in_ps counts_in_ps gaps_set egap_set tgate_set
            pos_set experts_set weights_set scattered first_sent rows_set head0_set
            ws_high_set ws_split x2t_low_set shared_in_ps tanh_set ga_set hp_set hs_high_set hs_set down_in_ps shared_added
            xst_in_ps xst_set gu_in_ps eth_set ega_set eh_set eht_in_ps eht_set y_in_ps ys_set
            choices_added first_added combined out_stored""".split()
        S = {n: sem(n) for n in names}
        x_in = [sem(f"x_in{c}") for c in range(T // G4)]
        xn2_saved = [sem(f"xn2_saved{c}") for c in range(2)]
        xs_in = [sem(f"xs_in{c}") for c in range(XS_RING)]
        ys_sent = [sem(f"ys_sent{c}") for c in range(YS_RING)]
        results_in = [[sem(f"{c}_in{q}") for c in ("first", "second")] for q in range(T // G4)]

        def g_ps(n):
            return quad[:, min(n, 1), :, :] if n < 2 * KD - 1 else result[:, :, :]

        def vt_ps(j):
            return (turned if j < 2 else result)[:, j % 2, 0:B * M]

        def vo_ps(n):
            return (turned if n % 2 else result)[:, 0, 0:D]

        def rows(ap):
            return ap.rearrange("b (p t) d -> p b t d", p=P)

        def tile_loop(eng, body):
            with eng.Fori(0, (LOOP1 - LOOP0) // 2) as i:
                for c in range(2):
                    body(i * 2 + (LOOP0 + c), c)

        ELOOP = (ET - 3) // XS_RING * XS_RING

        def expert_steps(eng, step):
            for t in range(XS_RING):
                step(t, t, 0, t // YS_RING, True)
            with eng.Fori(1, ELOOP // XS_RING) as i:
                for c in range(XS_RING):
                    step(i * XS_RING + c, c, i, i * (XS_RING // YS_RING) + c // YS_RING, False)
            for t in range(ELOOP, ET):
                step(t, t % XS_RING, t // XS_RING, t // YS_RING, True)

        def apart(eng):
            eng.wait_ge(S["filler_set"], 1)

        block = ctx.enter_context(nc.Block())

        @block.sync
        def _(sp):
            sp.dma_start(ctx_sb[:, :, :], ctx_t.rearrange("(k p) m -> p k m", p=P)).then_inc(S["kv_w_in"], 16)
            sp.dma_start(wk_sb[:, :, :], wk.rearrange("(k p) n -> p k n", p=P)).then_inc(S["kv_w_in"], 16)
            sp.dma_start(wqt_sb[:, :, :], wq_t.rearrange("(j p) n -> p j n", p=P)).then_inc(S["wq_in"], 16)
            sp.dma_start(wv_sb[:, :, :], wv.rearrange("(k p) n -> p k n", p=P)).then_inc(S["wv_in"], 16)
            sp.dma_start(wo_sb[:, :, :], wo.rearrange("(j p) n -> p j n", p=P)).then_inc(S["wo_in"], 16)
            for c in range(1, T // G4):
                b, tb = c * G4 // TB, c * G4 % TB
                sp.dma_start(x_all[:, c * G4:(c + 1) * G4, :], rows(x)[:, b, tb:tb + G4, :]).then_inc(x_in[c], 16)
            sp.dma_start(wr_sb[:, :, :], w_router.rearrange("(k p) n -> p k n", p=P)).then_inc(S["wr_in"], 16)
            sp.dma_start(ws_raw[:, 0:NI].rearrange("p (k n) -> p k n", k=KD), w_shared_in.rearrange("(k p) n -> p k n", p=P)).then_inc(S["ws_in"], 16)
            sp.dma_start(ws_raw[:, NI:].rearrange("p (j n) -> p j n", j=SJ), w_shared_out.rearrange("(j p) n -> p j n", p=P)).then_inc(S["ws_in"], 16)
            sp.wait_ge(S["filler_set"], 2)
            xs_rows = xs_dram.rearrange("(r p) d -> p r d", p=P)
            sp.dma_start(xs_rows[:, :, 0:D], filler[:, :].unsqueeze(1).to_broadcast([P, ET, D])).then_inc(S["rows_filled"], 16)
            sp.dma_start(xs_rows[:, :, D:XW], spare[:, :, :]).then_inc(S["rows_filled"], 16)

            def save(t, par):
                sp.wait_ge(S["xn2_set"], t + 1)
                sp.dma_start(xn2_all[:, t, 0:D], xn2[:, par, :]).then_inc(xn2_saved[par], 16)

            for t in range(LOOP0):
                save(t, t % 2)
            tile_loop(sp, save)
            sp.wait_ge(S["scores_in_ps"], T)
            sp.wait_ge(S["rows_filled"], 32)
            SHARE = E // (T - LOOP1)
            we_rows = w_expert.rearrange("e p n -> p e n")
            for t in range(LOOP1, T):
                save(t, t % 2)
                share = slice((t - LOOP1) * SHARE, (t - LOOP1 + 1) * SHARE)
                sp.dma_start(we_sb[:, share, :], we_rows[:, share, :]).then_inc(S["we_in"], 16)

            sp.wait_ge(S["scattered"], 16 * 2 * T)
            for t in range(XS_RING):
                sp.dma_start(xs[:, t, :], xs_dram[t * P:(t + 1) * P, :]).then_inc(xs_in[t], 16)

            def load(t, c, i, r, static):
                if not static or t + XS_RING < ET:
                    sp.wait_ge(ys_sent[c % YS_RING], (r + 1) * 16)
                    sp.dma_start(xs[:, c, :], xs_dram[bass.ds((t + XS_RING) * P, P), :]).then_inc(xs_in[c], 16)

            for t in range(XS_RING):
                load(t, t, 0, t // YS_RING, True)
            with sp.Fori(1, ELOOP // XS_RING - 1) as i:
                for c in range(XS_RING):
                    load(i * XS_RING + c, c, i, i * (XS_RING // YS_RING) + c // YS_RING, False)
            for t in range(ELOOP - XS_RING, ET):
                load(t, t % XS_RING, t // XS_RING, t // YS_RING, True)

            for slot in range(YS_RING):
                sp.wait_ge(ys_sent[slot], 16 * len(range(slot, ET, YS_RING)))
            for q in range(T // G4):
                for c, buf in enumerate((first, second)):
                    sp.dma_start(buf[:, q * G4:(q + 1) * G4, :],
                                 results_dram[c * T * P:(c + 1) * T * P, :].rearrange("(p t) d -> p t d", p=P)[
                                     :, q * G4:(q + 1) * G4, :]).then_inc(results_in[q][c], 16)

            out_rows = rows(out)
            stores = [(q * G4, G4) for q in range(T // G4 - 1)] + [(T - G4, G4 // 2), (T - G4 // 2, G4 // 2)]
            for n, (t, size) in enumerate(stores):
                sp.wait_ge(S["combined"], n + 1)
                b, tb = t // TB, t % TB
                sp.dma_start(out_rows[:, b, tb:tb + size, :], x_all[:, t:t + size, :]).then_inc(S["out_stored"], 16)
            sp.wait_ge(S["out_stored"], 16 * len(stores))

        @block.gpsimd
        def _(pool):
            link = [0]

            def linked(ins):
                link[0] += 1
                ins.then_inc(S["pool_link"], 1)
                pool.wait_ge(S["pool_link"], link[0])

            pool.memset(kt_sb[:, :, :, :, :], 0.0).then_inc(S["blocks_cleared"], 1)
            pool.memset(ident[:, :], 0.0).then_inc(S["ident_cleared"], 1)
            pool.memset(filler[:, :], 0.0).then_inc(S["filler_set"], 1)
            linked(pool.memset(spare[:, :, :], 0.0))
            pool.iota(spare[:, :, 0].bitcast(I32), pattern=[[P, ET]], base=2 * T * P, channel_multiplier=1).then_inc(S["filler_set"], 1)
            pool.wait_ge(S["ident_cleared"], 1)
            pool.affine_select(out=ident[:, :], in_=ident[:, :], compare_op=ALU.not_equal, fill=1.0, base=0,
                               pattern=[[-1, P]], channel_multiplier=1).then_inc(S["ident_set"], 1)
            pool.memset(vt_all[:, :], 0.0).then_inc(S["blocks_cleared"], 1)
            linked(pool.memset(head0[:, :], 0.0))
            pool.memset(head0[:, 0:M], 1.0).then_inc(S["head0_set"], 1)
            pool.memset(xn2_all[:, :, D:XW], 0.0).then_inc(S["rows_set"], 1)
            pool.iota(result_row[:, :], pattern=[[1, T]], base=0, channel_multiplier=T).then_inc(S["rows_set"], 1)

            def newton(t, par):
                v, hv, y, w = (z[:, par:par + 1] for z in (var2, half2, rstd2, newton2))
                pool.wait_ge(S["guess2_set"], t + 1)
                for s in range(NEWTON):
                    pool.tensor_tensor(w, y, y, ALU.mult)
                    if s == 0:
                        pool.tensor_scalar(hv, v, -0.5, None, ALU.mult)
                    pool.drain()
                    pool.tensor_scalar(w, w, hv, 1.5, ALU.mult, ALU.add)
                    pool.drain()
                    last = pool.tensor_tensor(y, y, w, ALU.mult)
                    if s < NEWTON - 1:
                        pool.drain()
                last.then_inc(S["rstd2_set"], 1)

            def normalize(t, par):
                pool.wait_ge(S["recip_set"], t + 1)
                p3 = probs[:, par, :].rearrange("p (h m) -> p h m", h=H)
                pool.tensor_tensor(p3, p3, srec[:, par, :].unsqueeze(2).to_broadcast([P, H, M]),
                                   ALU.mult).then_inc(S["probs_set"], 1)

            def split_low(n):
                raw, high, rest = ws_slices[n]
                pool.wait_ge(S["ws_high_set"], n + 1)
                pool.tensor_tensor(rest, raw, high.bitcast(F32), ALU.subtract).then_inc(S["ws_split"], 1)

            normalize(0, 0)
            pool.wait_ge(S["vo_in_ps"], B * KC)

            def step(t, par, static=False):
                if not static or t + 1 < T:
                    normalize(t + 1, 1 - par)
                if not static or 1 <= t <= T:
                    newton(t - 1, 1 - par)
                if static and t < LOOP0:
                    for n in SPLITS[t]:
                        split_low(n)

            for t in range(LOOP0):
                step(t, t % 2, True)
            tile_loop(pool, step)
            for t in range(LOOP1, T + 1):
                step(t, t % 2, True)

            linked(pool.iota(rank_first[:, :], pattern=[[-1, E]], base=E, channel_multiplier=0,
                             allow_small_or_imprecise_dtypes=True))
            pool.iota(step_rows[:, :], pattern=[[P, T]], base=0, channel_multiplier=0,
                      allow_small_or_imprecise_dtypes=True).then_inc(S["consts_set"], 1)
            pool.iota(tile_no[:, :], pattern=[[1, ET]], base=0, channel_multiplier=0,
                      allow_small_or_imprecise_dtypes=True).then_inc(S["consts_set"], 1)
            linked(pool.memset(before[:, :, :], 1.0))
            linked(pool.memset(earlier[:, :], 1.0))
            pool.memset(ones[:, :], 1.0).then_inc(S["consts_set"], 1)
            pool.affine_select(out=before[:, :, :], in_=before[:, :, :], compare_op=ALU.is_gt, fill=0.0, base=0,
                               pattern=[[1, E], [-1, E]], channel_multiplier=0).then_inc(S["consts_set"], 1)
            pool.affine_select(out=earlier[:, :], in_=earlier[:, :], compare_op=ALU.is_gt, fill=0.0, base=0,
                               pattern=[[1, P]], channel_multiplier=-1).then_inc(S["consts_set"], 1)

            for c in range(2):
                pool.wait_ge(xn2_saved[c], 16 * (T // 2))
            pool.wait_ge(S["rows_filled"], 32)
            pool.wait_ge(S["pos_set"], 1)
            for c in range(2):
                if c == 1:
                    pool.wait_ge(S["scattered"], 16 * T)
                if c == 0:
                    pool.wait_ge(S["rows_set"], 2)
                    pool.wait_ge(S["weights_set"], 1)
                pool.tensor_copy(xn2_all[:, :, D + 1], w12[:, c, :]).then_inc(S["rows_set"], 1)
                pool.tensor_scalar(xn2_all[:, :, D].bitcast(I32), result_row[:, :], float(c * T * P), None,
                                   ALU.add).then_inc(S["rows_set"], 1)
                pool.wait_ge(S["rows_set"], 2 * c + 4)
                for t in range(T):
                    pool.indirect_dma_start(xs_dram, bass.IndirectOffsetOnAxis(pos[:, c, t:t + 1], 0),
                                            xn2_all[:, t, :], None).then_inc(S["scattered"], 16)

            for t in range(ET):
                pool.wait_ge(S["ys_set"], t + 1)
                pool.indirect_dma_start(results_dram, bass.IndirectOffsetOnAxis(xs[:, t % XS_RING, D:D + 1].bitcast(U32), 0),
                                        ys[:, t % YS_RING, :], None).then_inc(ys_sent[t % YS_RING], 16)

            for q in range(ADDED):
                group = slice(q * G4, (q + 1) * G4)
                pool.wait_ge(results_in[q][0], 16)
                pool.wait_ge(results_in[q][1], 16)
                pool.tensor_tensor(first[:, group, :], first[:, group, :], second[:, group, :],
                                   ALU.add).then_inc(S["choices_added"], 1)

        @block.tensor
        def _(pe):
            mm, transpose = nc.tensor.matmul, nc.tensor.transpose

            def kv_t(w, ps_of, ready):
                for j in range(PAIRS):
                    for k in range(KD):
                        last = mm(ps_of(j), w[:, k, j * P:(j + 1) * P], ctx_sb[:, k, :],
                                  start=(k == 0), stop=(k == KD - 1))
                    last.then_inc(ready, 1)

            def fold_q(n):
                b, k = n // KD, n % KD
                if n == KD:
                    pe.wait_ge(S["g_set"], n)
                if n > KD:
                    pe.wait_ge(S["vo_set"], KC)
                for j in range(PAIRS):
                    c = (j % 2) * 2 * M
                    last = mm(g_ps(n)[:, j // 2, c:c + 2 * M], wqt_sb[:, j, k * P:(k + 1) * P],
                              kt_sb[:, j, b, :, :].rearrange("p a m -> p (a m)"), start=True, stop=True)
                last.then_inc(S["g_in_ps"], 1)

            def fold_o(b, slices=range(KC)):
                for c in slices:
                    n = b * KC + c
                    if n >= 2:
                        pe.wait_ge(S["vo_set"], n - 1)
                    pairs = [j for j in range(PAIRS) if j * 2 * M < c * P + KEYS[c] and (j + 1) * 2 * M > c * P]
                    for j in pairs:
                        last = mm(vo_ps(n)[0:KEYS[c], :], vt_sb[:, j, b, c * P:c * P + KEYS[c]], wo_sb[:, j, :],
                                  start=(j == pairs[0]), stop=(j == pairs[-1] and c > 0))
                    if c == 0:
                        last = mm(vo_ps(n)[0:KEYS[c], :], head0[:, :], bo_sb[:, :], start=False, stop=True)
                    last.then_inc(S["vo_in_ps"], 1)

            def turn_x(t, par, static=False):
                pe.wait_ge(S["xn1_set"], t + 1)
                if not static or t >= 3:
                    pe.wait_ge(S["pt_set"], t - 2)
                if static and 1 <= t < 3:
                    pe.wait_ge(S["xt_set"], t)
                for k in range(KD):
                    last = transpose(turned[:, 1, (k + 1) * P:(k + 2) * P], xn1[:, par, k * P:(k + 1) * P], ident[:, :])
                last.then_inc(S["xt_in_ps"], 1)

            def scores(t, par, static=False):
                pe.wait_ge(S["xt_set"], t + 1)
                if not static or t >= 2:
                    pe.wait_ge(S["shifted"], t - 1)
                for half in range(2):
                    for k in range(KD):
                        for a, b in PASSES:
                            last = mm(quad[:, par, half, 0:HALF], xt[a][:, par, k, :],
                                      gk[b][:, t // TB, k, half * HALF:(half + 1) * HALF],
                                      start=(k == 0 and (a, b) == PASSES[0]), stop=(k == KD - 1 and (a, b) == PASSES[-1]))
                last.then_inc(S["scores_in_ps"], 1)

            def turn_probs(t, par, static=False):
                pe.wait_ge(S["probs_set"], t + 1)
                if not static or t >= 1:
                    pe.wait_ge(S["pt_set"], t)
                if not static or t + 2 < T:
                    pe.wait_ge(S["xt_set"], t + 3)
                for c in range(KC):
                    last = transpose(turned_flat[0:KEYS[c], c * P:(c + 1) * P], probs[:, par, c * P:c * P + KEYS[c]], ident[:, :])
                last.then_inc(S["pt_in_ps"], 1)

            def attend(t, par, static=False):
                pe.wait_ge(S["pt_set"], t + 1)
                if not static or t >= 1:
                    pe.wait_ge(S["x2_set"], t)
                for c in range(KC):
                    last = mm(result_x, pt_sb[0:KEYS[c], c, :], vo_sb[0:KEYS[c], t // TB, c, :],
                              start=(c == 0), stop=(c == KC - 1))
                last.then_inc(S["attn_in_ps"], 1)

            def turn_xn2(t, par, static=False):
                pe.wait_ge(S["xn2_set"], t + 1)
                if not static or t >= 1:
                    pe.wait_ge(S["x2t_low_set"], t)
                for k in range(KD):
                    last = transpose(result[:, 1, k * P:(k + 1) * P], xn2[:, par, k * P:(k + 1) * P], ident[:, :])
                last.then_inc(S["xn2t_in_ps"], 1)

            pe.wait_ge(S["kv_w_in"], 32)
            kv_t(wk_sb, lambda j: quad[:, j // 2, j % 2, 0:B * M], S["kt_in_ps"])
            pe.wait_ge(S["wv_in"], 16)
            kv_t(wv_sb, vt_ps, S["vt_in_ps"])
            pe.wait_ge(S["wq_in"], 16)
            pe.wait_ge(S["kt_set"], 2 * PAIRS)
            fold_q(0)
            fold_q(1)
            pe.wait_ge(S["vt_set"], 2 * PAIRS)
            pe.wait_ge(S["wo_in"], 16)
            pe.wait_ge(S["bo_in"], 16)
            pe.wait_ge(S["head0_set"], 1)
            fold_o(0, range(2))
            pe.wait_ge(S["ident_set"], 1)
            turn_x(0, 0, True)
            turn_x(1, 1, True)
            pe.wait_ge(S["g_set"], KD)
            scores(0, 0, True)
            fold_q(2)
            fold_o(0, range(2, KC))
            turn_x(2, 0, True)
            fold_q(3)
            pe.wait_ge(S["g_set"], KD + 1)
            scores(1, 1, True)
            pe.wait_ge(S["g_set"], B * KD)
            fold_o(1)
            pe.wait_ge(S["vo_set"], B * KC)

            def step(t, par, static=False, meanwhile=None):
                turn_probs(t, par, static)
                if meanwhile:
                    meanwhile()
                if not static or t + 2 < T:
                    scores(t + 2, par, static)
                if not static or t + 3 < T:
                    turn_x(t + 3, 1 - par, static)
                attend(t, par, static)
                if not static or t >= 2:
                    turn_xn2(t - 2, par, static)

            def logits(g):
                pe.wait_ge(S["x2t_low_set"], G4 * (g + 1))
                if g >= 2:
                    pe.wait_ge(S["lt_set"], g - 1)
                for k in range(KD):
                    for a, b in PASSES:
                        last = mm(quad[0:NR, 1, g % 2, :], wr[a][:, k, :], x2t[b][:, k, g * GT:(g + 1) * GT],
                                  start=(k == 0 and (a, b) == PASSES[0]), stop=(k == KD - 1 and (a, b) == PASSES[-1]))
                last.then_inc(S["lt_in_ps"], 1)

            def turn_logits(g):
                pe.wait_ge(S["lt_set"], g + 1)
                for t in range(G4 * g, G4 * (g + 1)):
                    last = transpose(turned[:, 0, t * SCORE_W:t * SCORE_W + NR], lt_sb[:, t * P:(t + 1) * P], ident[0:NR, 0:NR])
                last.then_inc(S["logits_in_ps"], 1)

            def shared_in(g, slices=range(SJ)):
                for j in slices:
                    n = g * SJ + j
                    if n >= 4:
                        pe.wait_ge(S["hp_set"], n - 3)
                    for half in range(2):
                        c = half * SHID + j * P
                        for k in range(KD):
                            for a, b in PASSES:
                                last = mm(quad[:, n % 4 // 2, n % 2, half * ST:(half + 1) * ST], wsi[a][:, k, c:c + P],
                                          x2t[b][:, k, g * ST:(g + 1) * ST],
                                          start=(k == 0 and (a, b) == PASSES[0]), stop=(k == KD - 1 and (a, b) == PASSES[-1]))
                    last.then_inc(S["shared_in_ps"], 1)

            def shared_out(g):
                pe.wait_ge(S["hs_set"], (g + 1) * SJ)
                for t in range(SG):
                    n = g * SG + t
                    if n >= 2:
                        pe.wait_ge(S["shared_added"], n - 1)
                    for j in range(SJ):
                        for a, b in PASSES:
                            last = mm(result[:, t % 2, 0:D], hs[:, g % 2, a, j, t * P:(t + 1) * P], wso[b][:, j, :],
                                      start=(j == 0 and (a, b) == PASSES[0]), stop=(j == SJ - 1 and (a, b) == PASSES[-1]))
                    last.then_inc(S["down_in_ps"], 1)

            for t in range(LOOP0):
                step(t, t % 2, True)
            tile_loop(pe, step)
            for t in range(LOOP1, T - 1):
                step(t, t % 2, True)
            pe.wait_ge(S["ws_split"], len(ws_slices))
            pe.wait_ge(S["shifted"], T)
            step(T - 1, 1, True, meanwhile=lambda: logits(0))
            logits(1)
            shared_in(0, (0,))
            turn_xn2(T - 2, 0, True)
            logits(2)
            turn_logits(0)
            turn_logits(1)
            shared_in(0, (1,))
            turn_xn2(T - 1, 1, True)
            turn_logits(2)
            logits(3)
            turn_logits(3)
            shared_in(0, (2, 3))
            shared_in(1, (0, 1, 2))

            pe.wait_ge(S["consts_set"], 5)
            pe.wait_ge(S["picked_set"], 1)
            ranks = turned[:, 1, 0:T * E]
            mm(ranks, earlier[:, :], picked[:, :, :].rearrange("p t e -> p (t e)"), start=True, stop=False)
            for t in range(T - 1):
                later = T - 1 - t
                last = mm(turned[:, 1, (t + 1) * E:T * E].rearrange("p (t e) -> p t e", e=E), ones[:, :],
                          picked[:, t, :].unsqueeze(1).to_broadcast([P, later, E]), start=False, stop=(t == T - 2))
            last.then_inc(S["ranks_in_ps"], 1)
            pe.wait_ge(S["picked_t_set"], 1)
            mm(result[:, 1, 0:E], ones[:, :], picked_t[:, :], start=True, stop=True).then_inc(S["counts_in_ps"], 1)

            for g in range(1, NG_FIRST):
                shared_in(g, (3,) if g == 1 else range(SJ))
                shared_out(g - 1)
            shared_out(NG_FIRST - 1)


            def weights_at(t):
                return pe.value_load(expert_off[0:1, bass.ds(t, 1)], min_val=0, max_val=(E - 1) * EW)

            def turn_xs(t, slot, par, load_no):
                pe.wait_ge(xs_in[slot], load_no * 16)
                for k in range(KD):
                    last = transpose(turned[:, par, k * P:(k + 1) * P], xs[:, slot, k * P:(k + 1) * P], ident[:, :])
                last.then_inc(S["xst_in_ps"], 1)

            def expert_in(t, par, off):
                pe.wait_ge(S["xst_set"], t + 1)
                for k in range(KD):
                    last = mm(quad[:, 0, par, 0:2 * P], xst[:, par, k, :], we_flat[:, bass.ds(off + k * 2 * P, 2 * P)],
                              start=(k == 0), stop=(k == KD - 1))
                last.then_inc(S["gu_in_ps"], 1)

            def turn_h(t, par):
                pe.wait_ge(S["eh_set"], t + 1)
                transpose(quad[:, 1, par, 0:P], eh[:, par, :], ident[:, :]).then_inc(S["eht_in_ps"], 1)

            def expert_out(t, par, off, static=False):
                pe.wait_ge(S["eht_set"], t + 1)
                if not static or t >= 2:
                    pe.wait_ge(S["ys_set"], t - 1)
                mm(result[:, par, 0:D], eht[:, par, :], we_flat[:, bass.ds(off + KD * 2 * P, D)],
                   start=True, stop=True).then_inc(S["y_in_ps"], 1)

            pe.wait_ge(S["experts_set"], 1)
            pe.wait_ge(S["we_in"], 16 * (T - LOOP1))
            off0, off1 = weights_at(0), weights_at(1)
            turn_xs(0, 0, 0, 1)
            turn_xs(1, 1, 1, 1)
            expert_in(0, 0, off0)
            turn_xs(2, 2, 0, 1)
            expert_in(1, 1, off1)
            pe.wait_ge(S["shared_added"], NG_FIRST * SG)

            offs = {0: off0, 1: off1, 2: weights_at(2)}
            carried = [nc.alloc_registers(f"weights_at_{n}", engines=[mybir.EngineType.PE]) for n in range(3)]

            def expert_step(t, c, i, r, static):
                if c == 0 and not (static and t == 0):
                    for n in range(3):
                        offs[n] = nc.snap(carried[n], min_val=0, max_val=(E - 1) * EW)
                turn_h(t, c % 2)
                if not static or t + 3 < ET:
                    turn_xs(t + 3, (c + 3) % XS_RING, (c + 1) % 2, i + ((c + 3) // XS_RING + 1))
                if not static or t + 2 < ET:
                    expert_in(t + 2, c % 2, offs[c + 2])
                if not static or t + 3 < ET:
                    offs[c + 3] = weights_at(t + 3)
                expert_out(t, c % 2, offs[c], static)
                if c == XS_RING - 1:
                    for n in range(3):
                        nc.regs_mov(carried[n], offs[XS_RING + n])

            expert_steps(pe, expert_step)

            pe.wait_ge(S["ys_set"], ET)
            for g in range(NG_FIRST, NG):
                shared_in(g)
            for g in range(NG_FIRST, NG):
                shared_out(g)

        @block.scalar
        def _(act):
            copy = nc.scalar.copy
            act.dma_start(x_all[:, 0:G4, :], rows(x)[:, 0, 0:G4, :]).then_inc(x_in[0], 16)
            act.dma_start(bo_sb[:, :], bo.unsqueeze(0)).then_inc(S["bo_in"], 16)

            act.wait_ge(S["blocks_cleared"], 2)
            for j in range(PAIRS):
                act.wait_ge(S["vt_in_ps"], j + 1)
                for a in range(2):
                    q = slice(a * P // 2, (a + 1) * P // 2)
                    at = (2 * j + a) * M
                    copy(vt_sb[q, j, :, at:at + M],
                         vt_ps(j)[q, :].rearrange("p (b m) -> p b m", b=B)).then_inc(S["vt_set"], 1)

            def g_out(n):
                act.wait_ge(S["g_in_ps"], n + 1)
                copy(g_high[:, n // KD, n % KD, :].rearrange("p (a c) -> p a c", a=2),
                     g_ps(n)[:, :, 0:HALF]).then_inc(S["g_high_set"], 1)

            def xt_out(t, par, static=False):
                act.wait_ge(S["xt_in_ps"], t + 1)
                if not static or t >= 2:
                    act.wait_ge(S["scores_in_ps"], t - 1)
                copy(xt_high[:, par, :, :].rearrange("p k c -> p (k c)"), turned[:, 1, P:P + D]).then_inc(S["xt_high_set"], 1)

            def vo_out(n):
                act.wait_ge(S["vo_in_ps"], n + 1)
                b, c = n // KC, n % KC
                copy(vo_sb[0:KEYS[c], b, c, :], vo_ps(n)[0:KEYS[c], :]).then_inc(S["vo_set"], 1)

            def exps(t, par, static=False):
                act.wait_ge(S["shifted"], t + 1)
                nc.scalar.activation(probs[:, par, :], probs[:, par, :], ACT.Exp, scale=SCALE).then_inc(S["exps_set"], 1)

            g_out(0)
            g_out(1)
            vo_out(0)
            vo_out(1)
            xt_out(0, 0, True)
            xt_out(1, 1, True)
            g_out(2)
            vo_out(2)
            exps(0, 0)
            for c in range(3, KC):
                vo_out(c)
            xt_out(2, 0, True)
            g_out(3)
            for c in range(KC):
                vo_out(KC + c)

            def pt_out(t):
                act.wait_ge(S["pt_in_ps"], t + 1)
                copy(pt_sb[:, 0:KC - 1, :].rearrange("p c k -> p (c k)"), turned[:, 0, :])
                copy(pt_sb[0:KEYS[-1], KC - 1, :], turned[0:KEYS[-1], 1, 0:P]).then_inc(S["pt_set"], 1)

            def xn2t_out(t):
                act.wait_ge(S["xn2t_in_ps"], t + 1)
                copy(x2t_high[:, :, bass.ds(t * P, P)],
                     result[:, 1, 0:KD * P].rearrange("p (k c) -> p k c", k=KD)).then_inc(S["xn2t_set"], 1)

            def step(t, par, static=False):
                pt_out(t)
                if not static or t + 1 < T:
                    exps(t + 1, 1 - par)
                if not static or t + 3 < T:
                    xt_out(t + 3, 1 - par, static)
                if not static or t >= 2:
                    xn2t_out(t - 2)
                if static and t < LOOP0:
                    for n in SPLITS[t]:
                        split_high(n)

            def split_high(n):
                raw, high, _ = ws_slices[n]
                if n == 0:
                    act.wait_ge(S["ws_in"], 32)
                    act.wait_ge(S["wr_in"], 16)
                copy(high, raw).then_inc(S["ws_high_set"], 1)

            def logits_out(g):
                act.wait_ge(S["lt_in_ps"], g + 1)
                copy(lt_sb[:, g * GT:(g + 1) * GT], quad[0:NR, 1, g % 2, :]).then_inc(S["lt_set"], 1)

            for t in range(LOOP0):
                step(t, t % 2, True)
            tile_loop(act, step)
            for t in range(LOOP1, T):
                step(t, t % 2, True)
            def shared_tanh(n):
                act.wait_ge(S["shared_in_ps"], n + 1)
                if n >= 2:
                    act.wait_ge(S["ga_set"], n - 1)
                nc.scalar.activation(th[:, n % 2, :], quad[:, n % 4 // 2, n % 2, 0:ST], ACT.Tanh,
                                     scale=0.5).then_inc(S["tanh_set"], 1)

            def hs_high(n):
                g, j = n // SJ, n % SJ
                act.wait_ge(S["hp_set"], n + 1)
                if g >= 2:
                    act.wait_ge(S["down_in_ps"], (g - 1) * SG)
                copy(hs[:, g % 2, HIGH, j, :], hp[:, n % 2, :]).then_inc(S["hs_high_set"], 1)

            logits_out(0)
            logits_out(1)
            act.wait_ge(S["rows_filled"], 32)
            shared_tanh(0)
            xn2t_out(T - 2)
            logits_out(2)
            xn2t_out(T - 1)
            shared_tanh(1)
            hs_high(0)
            logits_out(3)
            hs_high(1)
            shared_tanh(2)
            shared_tanh(3)
            hs_high(2)
            act.wait_ge(S["gaps_set"], 1)
            nc.scalar.activation(tgate[:, :], lg[:, :, E], ACT.Tanh, scale=0.5).then_inc(S["tgate_set"], 1)
            nc.scalar.activation(egap[:, :], gap[:, :], ACT.Exp).then_inc(S["egap_set"], 1)
            for n in range(4, NG_FIRST * SJ):
                shared_tanh(n)
                hs_high(n - 1)
            hs_high(NG_FIRST * SJ - 1)

            def xst_out(t, par, static=False):
                act.wait_ge(S["xst_in_ps"], t + 1)
                if not static or t >= 2:
                    act.wait_ge(S["gu_in_ps"], t - 1)
                copy(xst[:, par, :, :].rearrange("p k c -> p (k c)"), turned[:, par, 0:D]).then_inc(S["xst_set"], 1)

            def expert_tanh(t, par, static=False):
                act.wait_ge(S["gu_in_ps"], t + 1)
                if not static or t >= 2:
                    act.wait_ge(S["ega_set"], t - 1)
                nc.scalar.activation(eth[:, par, :], quad[:, 0, par, 0:P], ACT.Tanh,
                                     scale=0.5).then_inc(S["eth_set"], 1)

            def y_out(t, c, r, static):
                act.wait_ge(S["y_in_ps"], t + 1)
                if not static or t >= YS_RING:
                    act.wait_ge(ys_sent[c % YS_RING], r * 16)
                nc.scalar.activation(ys[:, c % YS_RING, :], result[:, c % 2, 0:D], ACT.Copy,
                                     scale=xs[:, c, D + 1:D + 2]).then_inc(S["ys_set"], 1)

            xst_out(0, 0, True)
            xst_out(1, 1, True)
            expert_tanh(0, 0, True)
            xst_out(2, 0, True)
            expert_tanh(1, 1, True)

            def expert_step(t, c, i, r, static):
                if not static or t + 3 < ET:
                    xst_out(t + 3, (c + 1) % 2)
                if not static or t + 2 < ET:
                    expert_tanh(t + 2, c % 2)
                y_out(t, c, r, static)

            expert_steps(act, expert_step)

            shared_tanh(NG_FIRST * SJ)
            for n in range(NG_FIRST * SJ + 1, NG * SJ):
                shared_tanh(n)
                hs_high(n - 1)
            hs_high(NG * SJ - 1)

        @block.vector
        def _(dve):
            v = nc.vector
            link = [0]

            def marked(ins):
                link[0] += 1
                ins.then_inc(S["dve_link"], 1)

            def wait_marked():
                dve.wait_ge(S["dve_link"], link[0])

            def linked(ins):
                marked(ins)
                wait_marked()

            dve.wait_ge(S["blocks_cleared"], 1)
            for j in range(PAIRS):
                dve.wait_ge(S["kt_in_ps"], j + 1)
                for a in range(2):
                    q = slice(a * P // 2, (a + 1) * P // 2)
                    v.tensor_copy(kt_sb[q, j, :, a, :],
                                  quad[q, j // 2, j % 2, 0:B * M].rearrange("p (b m) -> p b m", b=B)).then_inc(S["kt_set"], 1)

            def norm1_stats(t0, t1):
                for t in range(t0, t1):
                    if t % G4 == 0:
                        dve.wait_ge(x_in[t // G4], 16)
                    ins = v.bn_stats(stats[:, t, :], x_all[:, t, :])
                return ins

            def norm1(t0, t1, stats_end):
                linked(stats_end)
                for t in range(t0, t1):
                    ins = v.bn_aggr(moments1[:, t, :], stats[:, t, :])
                linked(ins)
                va, y, w = (z[:, t0:t1] for z in (var1, rstd1, newton1))
                linked(v.tensor_scalar(va, moments1[:, t0:t1, 1], LN_EPS, None, ALU.add))
                linked(v.tensor_scalar(w.bitcast(I32), va.bitcast(I32), 1, None, ALU.logical_shift_right))
                linked(v.tensor_scalar(y.bitcast(I32), w.bitcast(I32), -1.0, float(RSQRT_MAGIC), ALU.mult, ALU.add))
                for _ in range(NEWTON):
                    linked(v.tensor_tensor(w, y, y, ALU.mult))
                    linked(v.scalar_tensor_tensor(w, w, -0.5, va, ALU.mult, ALU.mult))
                    linked(v.scalar_tensor_tensor(y, w, 1.5, y, ALU.add, ALU.mult))

            def apply1(t, par, static=False):
                if not static or t >= 2:
                    dve.wait_ge(S["xt_in_ps"], t - 1)
                tt = bass.ds(t, 1)
                v.tensor_scalar(xn1[:, par, :], x_all[:, t, :], moments1[:, t, 0:1], rstd1[:, tt],
                                ALU.subtract, ALU.mult).then_inc(S["xn1_set"], 1)

            def g_rest(n):
                dve.wait_ge(S["g_high_set"], n + 1)
                half = lambda w: w[:, n // KD, n % KD, :].rearrange("p (a c) -> p a c", a=2)
                v.tensor_tensor(half(g_low), g_ps(n)[:, :, 0:HALF], half(g_high).bitcast(F32),
                                ALU.subtract).then_inc(S["g_set"], 1)

            def xt_rest(t, par):
                dve.wait_ge(S["xt_high_set"], t + 1)
                flat = lambda w: w[:, par, :, :].rearrange("p k c -> p (k c)")
                v.tensor_tensor(flat(xt_low), turned[:, 1, P:P + D], flat(xt_high).bitcast(F32),
                                ALU.subtract).then_inc(S["xt_set"], 1)

            def maxima(t, par):
                dve.wait_ge(S["scores_in_ps"], t + 1)
                v.tensor_reduce(smax[:, par, :].rearrange("p (a h) -> p a h", a=2),
                                quad[:, par, :, 0:HALF].rearrange("p a (h m) -> p a h m", h=HH), AX,
                                ALU.max).then_inc(S["max_found"], 1)

            def shift(t, par, static=False):
                dve.wait_ge(S["max_found"], t + 1)
                if not static or t >= 2:
                    dve.wait_ge(S["pt_in_ps"], t - 1)
                v.tensor_tensor(probs[:, par, :].rearrange("p (a h m) -> p a h m", a=2, h=HH),
                                quad[:, par, :, 0:HALF].rearrange("p a (h m) -> p a h m", h=HH),
                                smax[:, par, :].rearrange("p (a h) -> p a h", a=2).unsqueeze(3).to_broadcast([P, 2, HH, M]),
                                ALU.subtract).then_inc(S["shifted"], 1)

            def sums(t, par):
                dve.wait_ge(S["exps_set"], t + 1)
                v.tensor_reduce(ssum[:, par, :], probs[:, par, :].rearrange("p (h m) -> p h m", h=H), AX,
                                ALU.add).then_inc(S["summed"], 1)

            def invert(t, par):
                dve.wait_ge(S["summed"], t + 1)
                v.reciprocal(srec[:, par, :], ssum[:, par, :]).then_inc(S["recip_set"], 1)

            norm1(0, G4, norm1_stats(0, G4))
            apply1(0, 0, True)
            g_rest(0)
            apply1(1, 1, True)
            g_rest(1)
            xt_rest(0, 0)
            apply1(2, 0, True)
            norm1_stats(G4, G4 + 2)
            xt_rest(1, 1)
            norm1_stats(G4 + 2, G4 + 4)
            maxima(0, 0)
            shift(0, 0, True)
            g_rest(2)
            sums(0, 0)
            norm1_stats(2 * G4, 2 * G4 + 2)
            invert(0, 0)
            norm1_stats(2 * G4 + 2, T - 2)
            xt_rest(2, 0)
            g_rest(3)
            norm1(G4, T, norm1_stats(T - 2, T))

            def residual(t):
                dve.wait_ge(S["attn_in_ps"], t + 1)
                v.tensor_tensor(x_all[:, t, :], result_x, x_all[:, t, :], ALU.add).then_inc(S["x2_set"], 1)

            def norm2_stats(t):
                apart(dve)
                dve.wait_ge(S["x2_set"], t + 1)
                v.bn_stats(stats2[:, :], x_all[:, t, :]).then_inc(S["stats2_set"], 1)

            def norm2_moments(t, par):
                apart(dve)
                dve.wait_ge(S["stats2_set"], t + 1)
                v.bn_aggr(moments2[:, par, :], stats2[:, :]).then_inc(S["moments2_set"], 1)

            def norm2_var(t, par):
                dve.wait_ge(S["moments2_set"], t + 1)
                v.tensor_scalar(var2[:, par:par + 1], moments2[:, par, 1:2], LN_EPS, None,
                                ALU.add).then_inc(S["var2_set"], 1)

            def norm2_halve(t, par):
                dve.wait_ge(S["var2_set"], t + 1)
                v.tensor_scalar(newton2[:, par:par + 1].bitcast(I32), var2[:, par:par + 1].bitcast(I32), 1, None,
                                ALU.logical_shift_right).then_inc(S["halved2_set"], 1)

            def norm2_guess(t, par):
                dve.wait_ge(S["halved2_set"], t + 1)
                v.tensor_scalar(rstd2[:, par:par + 1].bitcast(I32), newton2[:, par:par + 1].bitcast(I32), -1.0,
                                float(RSQRT_MAGIC), ALU.mult, ALU.add).then_inc(S["guess2_set"], 1)

            def apply2(t, par, static=False):
                dve.wait_ge(S["rstd2_set"], t + 1)
                if not static or t >= 2:
                    dve.wait_ge(S["xn2t_in_ps"], t - 1)
                    dve.wait_ge(xn2_saved[par], 8 * (t - par))
                v.tensor_scalar(xn2[:, par, :], x_all[:, t, :], moments2[:, par, 0:1], rstd2[:, par:par + 1],
                                ALU.subtract, ALU.mult).then_inc(S["xn2_set"], 1)

            def x2t_rest(t):
                dve.wait_ge(S["xn2t_set"], t + 1)
                tile = bass.ds(t * P, P)
                v.tensor_tensor(x2t_low[:, :, tile], result[:, 1, 0:KD * P].rearrange("p (k c) -> p k c", k=KD),
                                x2t_high[:, :, tile].bitcast(F32), ALU.subtract).then_inc(S["x2t_low_set"], 1)

            def step(t, par, static=False):
                other = 1 - par
                softmax = not static or t + 1 < T
                second = not static or 1 <= t <= T
                ahead = not static or t + 3 < T
                if softmax:
                    maxima(t + 1, other)
                if ahead:
                    apply1(t + 3, other, static)
                if softmax:
                    shift(t + 1, other, static)
                if second:
                    residual(t - 1)
                if not static or 3 <= t <= T:
                    x2t_rest(t - 3)
                if second:
                    norm2_stats(t - 1)
                if softmax:
                    sums(t + 1, other)
                if second:
                    norm2_moments(t - 1, other)
                if softmax:
                    invert(t + 1, other)
                if second:
                    norm2_var(t - 1, other)
                if ahead:
                    xt_rest(t + 3, other)
                if second:
                    norm2_halve(t - 1, other)
                if not static or t >= 2:
                    apply2(t - 2, par, static)
                if second:
                    norm2_guess(t - 1, other)

            for t in range(LOOP0):
                step(t, t % 2, True)
            tile_loop(dve, step)
            def shared_h(n, start=False):
                gate_h(n)
                up_h(n)
                if not start:
                    hs_rest(n - 1)

            def gate_h(n):
                dve.wait_ge(S["tanh_set"], n + 1)
                v.scalar_tensor_tensor(ga[:, n % 2, :], th[:, n % 2, :], 1.0, quad[:, n % 4 // 2, n % 2, 0:ST], ALU.add,
                                       ALU.mult).then_inc(S["ga_set"], 1)

            def up_h(n):
                dve.wait_ge(S["ga_set"], n + 1)
                if n >= 2:
                    dve.wait_ge(S["hs_high_set"], n - 1)
                    dve.wait_ge(S["hs_set"], n - 1)
                v.tensor_tensor(hp[:, n % 2, :], ga[:, n % 2, :], quad[:, n % 4 // 2, n % 2, ST:2 * ST],
                                ALU.mult).then_inc(S["hp_set"], 1)

            def hs_rest(n):
                g, j = n // SJ, n % SJ
                dve.wait_ge(S["hs_high_set"], n + 1)
                if g >= 2:
                    dve.wait_ge(S["down_in_ps"], (g - 1) * SG)
                v.tensor_tensor(hs[:, g % 2, LOW, j, :], hp[:, n % 2, :], hs[:, g % 2, HIGH, j, :].bitcast(F32),
                                ALU.subtract).then_inc(S["hs_set"], 1)

            for t in range(LOOP1, T + 1):
                step(t, t % 2, True)
            shared_h(0, True)
            apply2(T - 1, 1, True)
            x2t_rest(T - 2)
            x2t_rest(T - 1)
            shared_h(1)

            def te(z):
                return z.unsqueeze(2).to_broadcast([P, T, E])

            first_rank = rank_first[:, :].unsqueeze(1).to_broadcast([P, T, E])
            dve.wait_ge(S["logits_in_ps"], T // G4)
            linked(v.tensor_copy(lg[:, :, :], turned[:, 0, 0:T * SCORE_W].rearrange("p (t n) -> p t n", n=SCORE_W)[:, :, 0:NR]))
            dve.wait_ge(S["consts_set"], 5)

            def choose(l, top, oh, n):
                linked(v.tensor_reduce(top, l, AX, ALU.max))
                linked(v.tensor_tensor(eq[:, :, :], l, te(top), ALU.is_equal))
                linked(v.tensor_tensor(eq[:, :, :], eq[:, :, :], first_rank, ALU.mult))
                marked(v.tensor_reduce(pick[:, :], eq[:, :, :], AX, ALU.max))
                gate_h(n)
                wait_marked()
                marked(v.tensor_tensor(oh, eq[:, :, :], te(pick[:, :]), ALU.is_equal))
                up_h(n)
                wait_marked()

            choose(lg[:, :, 0:E], top1[:, :], oh1[:, :, :], 2)
            marked(v.scalar_tensor_tensor(lg2[:, :, :], oh1[:, :, :], MASKED, lg[:, :, 0:E], ALU.mult, ALU.add))
            hs_rest(1)
            wait_marked()
            choose(lg2[:, :, :], top2[:, :], oh2[:, :, :], 3)
            v.tensor_tensor(gap[:, :], top2[:, :], top1[:, :], ALU.subtract).then_inc(S["gaps_set"], 1)
            v.tensor_tensor(picked[:, :, :], oh1[:, :, :], oh2[:, :, :], ALU.add).then_inc(S["picked_set"], 1)
            hs_rest(2)
            dve.wait_ge(S["picked_set"], 1)
            with nc.allow_low_precision(reason="counts up to 16 are exact in bfloat16"):
                v.tensor_reduce(picked_t[:, :], picked[:, :, :].rearrange("p t e -> p e t"), AX, ALU.add).then_inc(S["picked_t_set"], 1)

            dve.wait_ge(S["egap_set"], 1)
            linked(v.tensor_scalar(gap[:, :], egap[:, :], 2.0, 2.0, ALU.mult, ALU.add))
            linked(v.reciprocal(w12[:, 0, :], gap[:, :]))
            v.tensor_tensor(w12[:, 1, :], w12[:, 0, :], egap[:, :], ALU.mult).then_inc(S["weights_set"], 1)

            dve.wait_ge(S["counts_in_ps"], 1)
            linked(v.tensor_copy(counts[:, :], result[:, 1, 0:E]))
            marked(v.tensor_tensor(eq[:, 0:E, :], counts[:, :].unsqueeze(2).to_broadcast([P, E, T]),
                                   step_rows[:, :].unsqueeze(1).to_broadcast([P, E, T]), ALU.is_gt))
            hs_rest(3)
            wait_marked()
            marked(v.tensor_reduce(ntiles[:, :], eq[:, 0:E, :], AX, ALU.add))
            gate_h(4)
            wait_marked()
            marked(v.tensor_tensor(lg2[:, 0:E, :], before[:, :, :], ntiles[:, :].unsqueeze(1).to_broadcast([P, E, E]), ALU.mult))
            up_h(4)
            wait_marked()
            marked(v.tensor_reduce(base[:, :], lg2[:, 0:E, :], AX, ALU.add))
            gate_h(5)
            wait_marked()
            marked(v.tensor_scalar(base_row[:, :], base[:, :], float(P), None, ALU.mult))
            up_h(5)
            wait_marked()
            linked(v.tensor_tensor(lg2[:, :, :], turned[:, 1, 0:T * E].rearrange("p (t e) -> p t e", e=E),
                                   base_row[:, :].unsqueeze(1).to_broadcast([P, T, E]), ALU.add))
            for c, oh in enumerate((oh1, oh2)):
                linked(v.tensor_tensor(eq[:, :, :], oh[:, :, :], lg2[:, :, :], ALU.mult))
                linked(v.tensor_reduce(posf[:, c, :], eq[:, :, :], AX, ALU.add))
            v.tensor_copy(pos[:, :, :], posf[:, :, :]).then_inc(S["pos_set"], 1)
            hs_rest(4)
            for n in range(6, 2 * SJ):
                shared_h(n)
            dve.wait_ge(S["tgate_set"], 1)
            linked(v.tensor_scalar(sgate[:, :], tgate[:, :], 0.25, 0.25, ALU.mult, ALU.add))

            def add_shared(t):
                dve.wait_ge(S["down_in_ps"], t + 1)
                v.scalar_tensor_tensor(x_all[:, t, :], result[:, t % 2, 0:D], sgate[:, t:t + 1],
                                       x_all[:, t, :], ALU.mult, ALU.add).then_inc(S["shared_added"], 1)

            def experts_of_tiles():
                linked(v.tensor_tensor(base_end[:, :], base[:, :], ntiles[:, :], ALU.add))
                linked(v.tensor_tensor(past[:, :, :], base_end[0:1, :].unsqueeze(1).to_broadcast([1, ET, E]),
                                       tile_no[:, :].unsqueeze(2).to_broadcast([1, ET, E]), ALU.is_le))
                linked(v.tensor_reduce(ewf[:, :], past[:, :, :], AX, ALU.add))
                linked(v.tensor_scalar(ewf[:, :], ewf[:, :], float(E - 1), float(EW), ALU.min, ALU.mult))
                v.tensor_copy(expert_off[:, :], ewf[:, :]).then_inc(S["experts_set"], 1)

            for g in range(1, NG_FIRST):
                if g == NG_FIRST // 2:
                    experts_of_tiles()
                for n in range(max(2, g) * SJ, (g + 1) * SJ):
                    shared_h(n)
                if g == NG_FIRST - 1:
                    hs_rest(NG_FIRST * SJ - 1)
                for t in range((g - 1) * SG, g * SG):
                    add_shared(t)
            for t in range((NG_FIRST - 1) * SG, NG_FIRST * SG):
                add_shared(t)

            def expert_h(t, par, static=False):
                dve.wait_ge(S["eth_set"], t + 1)
                v.scalar_tensor_tensor(ega[:, par, :], eth[:, par, :], 1.0, quad[:, 0, par, 0:P], ALU.add,
                                       ALU.mult).then_inc(S["ega_set"], 1)
                dve.wait_ge(S["ega_set"], t + 1)
                if not static or t >= 2:
                    dve.wait_ge(S["eht_in_ps"], t - 1)
                v.tensor_tensor(eh[:, par, :], ega[:, par, :], quad[:, 0, par, P:2 * P], ALU.mult).then_inc(S["eh_set"], 1)

            def eht_out(t, par, static=False):
                dve.wait_ge(S["eht_in_ps"], t + 1)
                if not static or t >= 2:
                    dve.wait_ge(S["y_in_ps"], t - 1)
                v.tensor_copy(eht[:, par, :], quad[:, 1, par, 0:P]).then_inc(S["eht_set"], 1)

            expert_h(0, 0, True)
            expert_h(1, 1, True)

            def expert_step(t, c, i, r, static):
                eht_out(t, c % 2, static)
                if not static or t + 2 < ET:
                    expert_h(t + 2, c % 2)

            expert_steps(dve, expert_step)

            def combine(t, size, results):
                v.tensor_tensor(x_all[:, t:t + size, :], x_all[:, t:t + size, :], results[:, t:t + size, :],
                                ALU.add).then_inc(S["combined"], 1)

            def combine_group(q):
                dve.wait_ge(S["choices_added"], q + 1)
                dve.wait_ge(S["shared_added"], (q + 1) * G4)
                combine(q * G4, G4, first)

            shared_h(NG_FIRST * SJ, True)
            for n in range(NG_FIRST * SJ + 1, NG * SJ):
                shared_h(n)
            hs_rest(NG * SJ - 1)
            for q in range(ADDED):
                combine_group(q)
                if q < SG:
                    add_shared(NG_FIRST * SG + q)
            dve.wait_ge(S["shared_added"], T)
            dve.wait_ge(results_in[ADDED][0], 16)
            v.tensor_tensor(x_all[:, T - G4:T, :], x_all[:, T - G4:T, :], first[:, T - G4:T, :], ALU.add).then_inc(S["first_added"], 1)
            dve.wait_ge(results_in[ADDED][1], 16)
            dve.wait_ge(S["first_added"], 1)
            combine(T - G4, G4 // 2, second)
            combine(T - G4 // 2, G4 // 2, second)


def kernel(**inputs):
    import numpy as np
    import concourse.bacc as bacc
    from concourse.bass_utils import run_bass_kernel_spmd

    a = {k: np.asarray(v) for k, v in inputs.items()}
    x, c = a["x"], a["ctx_1024"]
    B, N, D = x.shape
    M = c.shape[1]
    gate, up, down = a["L0_ffn_We_gate"], a["L0_ffn_We_up"], a["L0_ffn_We_down"]
    E, HID, _ = gate.shape
    KD = D // P
    gu = np.concatenate([gate, up], axis=1).transpose(0, 2, 1).reshape(E, KD, P, 2 * HID)
    w_expert = np.concatenate([gu[:, k] for k in range(KD)] + [down.transpose(0, 2, 1)], axis=2)
    arrays = {
        "x": x,
        "ctx_t": c.transpose(2, 0, 1).reshape(D, B * M),
        "wk": a["L0_xattn_Wk"],
        "wv": a["L0_xattn_Wv"],
        "wq_t": a["L0_xattn_Wq"].T,
        "wo": a["L0_xattn_Wo"],
        "bo": a["L0_xattn_bo"],
        "w_router": np.concatenate([a["L0_ffn_Wg"], a["L0_ffn_Wsg"]], axis=0).T,
        "w_expert": w_expert,
        "w_shared_in": np.concatenate([a["L0_ffn_Ws_gate"], a["L0_ffn_Ws_up"]], axis=0).T,
        "w_shared_out": a["L0_ffn_Ws_down"].T,
    }
    nc = bacc.Bacc("TRN2", target_bir_lowering=False, num_devices=1)
    named, args = {}, []
    for name, v in arrays.items():
        v = np.ascontiguousarray(v)
        named[f"in_{name}"] = v
        args.append(nc.dram_tensor(f"in_{name}", v.shape, mybir.dt.from_np(v.dtype), kind="ExternalInput").ap())
    args.append(nc.dram_tensor("out_x", (B, N, D), F32, kind="ExternalOutput").ap())
    build(nc, *args)
    r = run_bass_kernel_spmd(nc, [named], core_ids=[0])
    return r.results[0]["out_x"]
```
